# Optimizing a Trainium2 kernel written in Bass

```python
import numpy as np
import jax
import jax.numpy as jnp

def _softmax(x, axis=-1):
    return jax.nn.softmax(x, axis=axis)

def _gelu(x):
    return jax.nn.gelu(x, approximate=True)

def _silu(x):
    return jax.nn.silu(x)

def _sigmoid(x):
    return jax.nn.sigmoid(x)

def _layernorm(x, axis=-1, eps=1e-05):
    m = jnp.mean(x, axis=axis, keepdims=True)
    v = jnp.var(x, axis=axis, keepdims=True)
    return (x - m) / jnp.sqrt(v + eps)

def _scatter_add(tgt, idx, src, axis=0):
    return tgt.at[idx].add(src)

def _segment_sum(src, seg, n):
    return jax.ops.segment_sum(src, seg, n)
kernel_name = 'mk_recurrent_d1_jaxref_r8_b4e00b'

def setup_inputs(seed: int=0):
    np.random.seed(seed)
    _w = jnp.asarray

    def _L0_attn_setup():
        import jax, jax.numpy as jnp
        import numpy as np
        D_MODEL = 128
        STATE = 64
        HEADS = 8
        EXPAND = 2
        INNER = EXPAND * D_MODEL
        HEAD_DIM = INNER // HEADS
        PROJ_OUT = 2 * INNER + 2 * STATE + HEADS
        BATCH, SEQ = (2, 128)
        EPS = 1e-05

        def _layer_norm(x, gamma, beta):
            mu = jnp.mean(x, axis=-1, keepdims=True)
            xc = x - mu
            var = jnp.mean(xc * xc, axis=-1, keepdims=True)
            return xc * jax.lax.rsqrt(var + EPS) * gamma + beta

        def _mamba2(u, W_in, b_in, A_log, D_skip, dt_bias, W_out, b_out):
            B, L, _ = u.shape
            zxbcdt = u @ W_in + b_in
            z = zxbcdt[..., :INNER]
            xs = zxbcdt[..., INNER:2 * INNER].reshape(B, L, HEADS, HEAD_DIM)
            Bm = zxbcdt[..., 2 * INNER:2 * INNER + STATE]
            Cm = zxbcdt[..., 2 * INNER + STATE:2 * INNER + 2 * STATE]
            dt = jax.nn.softplus(zxbcdt[..., 2 * INNER + 2 * STATE:] + dt_bias)
            A = -jnp.exp(A_log)
            decay = jnp.exp(dt * A)
            dtx = dt[..., None] * xs

            def step(h, inp):
                dec_t, dtx_t, B_t, C_t = inp
                h = dec_t[:, :, None, None] * h + dtx_t[..., None] * B_t[:, None, None, :]
                y = jnp.einsum('bhpn,bn->bhp', h, C_t)
                return (h, y)
            h0 = jnp.zeros((B, HEADS, HEAD_DIM, STATE), u.dtype)
            scan_in = (jnp.moveaxis(decay, 1, 0), jnp.moveaxis(dtx, 1, 0), jnp.moveaxis(Bm, 1, 0), jnp.moveaxis(Cm, 1, 0))
            _, ys = jax.lax.scan(step, h0, scan_in)
            y = jnp.moveaxis(ys, 0, 1)
            y = y + D_skip[None, None, :, None] * xs
            y = y.reshape(B, L, INNER) * jax.nn.silu(z)
            return y @ W_out + b_out
        key = jax.random.key(seed)
        ks = jax.random.split(key, 6)
        g = lambda k, shape, sc: jax.random.normal(k, shape, jnp.float32) * sc
        return {'input_tensor': jax.random.normal(ks[0], (BATCH, SEQ, D_MODEL), jnp.float32), 'ln_gamma': jnp.ones((D_MODEL,), jnp.float32), 'ln_beta': jnp.zeros((D_MODEL,), jnp.float32), 'W_in': g(ks[1], (D_MODEL, PROJ_OUT), 0.02), 'b_in': jnp.zeros((PROJ_OUT,), jnp.float32), 'A_log': jnp.log(jnp.arange(1, HEADS + 1, dtype=jnp.float32)), 'D_skip': jnp.ones((HEADS,), jnp.float32), 'dt_bias': g(ks[2], (HEADS,), 0.1), 'W_out': g(ks[3], (INNER, D_MODEL), 0.02), 'b_out': jnp.zeros((D_MODEL,), jnp.float32)}
    _L0_attn_in = _L0_attn_setup()

    def _L0_ffn_setup():
        import jax, jax.numpy as jnp
        import numpy as np
        DIM = 128

        def _reference_tuple_inner(x, W_r, W_k, W_v, mu_r, mu_k):
            B, T, C = x.shape
            x_prev = jnp.concatenate([jnp.zeros((B, 1, C), x.dtype), x[:, :-1, :]], axis=1)
            xr = mu_r * x + (1.0 - mu_r) * x_prev
            xk = mu_k * x + (1.0 - mu_k) * x_prev
            r = jax.nn.sigmoid(jnp.einsum('btc,dc->btd', xr, W_r))
            k = jnp.einsum('btc,dc->btd', xk, W_k)
            k_act = jnp.square(jax.nn.relu(k))
            out = r * jnp.einsum('btc,dc->btd', k_act, W_v)
            new_state = x[:, -1, :]
            return (out, new_state)
        key = jax.random.key(seed)
        ks = jax.random.split(key, 6)
        B, T, C = (8, 256, DIM)
        x = jax.random.normal(ks[0], (B, T, C), dtype=jnp.float32)
        s = 1.0 / np.sqrt(C)
        W_r = jax.random.uniform(ks[1], (C, C), jnp.float32, -s, s)
        W_k = jax.random.uniform(ks[2], (C, C), jnp.float32, -s, s)
        W_v = jax.random.uniform(ks[3], (C, C), jnp.float32, -s, s)
        mu_r = jax.random.uniform(ks[4], (C,), jnp.float32)
        mu_k = jax.random.uniform(ks[5], (C,), jnp.float32)
        return {'x': x, 'W_r': W_r, 'W_k': W_k, 'W_v': W_v, 'mu_r': mu_r, 'mu_k': mu_k}
    _L0_ffn_in = _L0_ffn_setup()
    _d = {'L0_attn_input_tensor': _L0_attn_in['input_tensor'], 'L0_attn_ln_gamma': _L0_attn_in['ln_gamma'], 'L0_attn_ln_beta': _L0_attn_in['ln_beta'], 'L0_attn_W_in': _L0_attn_in['W_in'], 'L0_attn_b_in': _L0_attn_in['b_in'], 'L0_attn_A_log': _L0_attn_in['A_log'], 'L0_attn_D_skip': _L0_attn_in['D_skip'], 'L0_attn_dt_bias': _L0_attn_in['dt_bias'], 'L0_attn_W_out': _L0_attn_in['W_out'], 'L0_attn_b_out': _L0_attn_in['b_out'], 'L0_ffn_W_r': _L0_ffn_in['W_r'], 'L0_ffn_W_k': _L0_ffn_in['W_k'], 'L0_ffn_W_v': _L0_ffn_in['W_v'], 'L0_ffn_mu_r': _L0_ffn_in['mu_r'], 'L0_ffn_mu_k': _L0_ffn_in['mu_k']}
    _x0 = _d['L0_attn_input_tensor']
    _d['L0_attn_input_tensor'] = jax.random.normal(jax.random.fold_in(jax.random.key(seed), 1), (32, 256, 128), dtype=_x0.dtype)
    del _x0
    return _d

def reference(L0_attn_input_tensor, L0_attn_ln_gamma, L0_attn_ln_beta, L0_attn_W_in, L0_attn_b_in, L0_attn_A_log, L0_attn_D_skip, L0_attn_dt_bias, L0_attn_W_out, L0_attn_b_out, L0_ffn_W_r, L0_ffn_W_k, L0_ffn_W_v, L0_ffn_mu_r, L0_ffn_mu_k):

    def _L0_attn_ref(input_tensor, ln_gamma, ln_beta, W_in, b_in, A_log, D_skip, dt_bias, W_out, b_out):
        import jax, jax.numpy as jnp
        import numpy as np
        D_MODEL = 128
        STATE = 64
        HEADS = 8
        EXPAND = 2
        INNER = EXPAND * D_MODEL
        HEAD_DIM = INNER // HEADS
        PROJ_OUT = 2 * INNER + 2 * STATE + HEADS
        BATCH, SEQ = (2, 128)
        EPS = 1e-05

        def _layer_norm(x, gamma, beta):
            mu = jnp.mean(x, axis=-1, keepdims=True)
            xc = x - mu
            var = jnp.mean(xc * xc, axis=-1, keepdims=True)
            return xc * jax.lax.rsqrt(var + EPS) * gamma + beta

        def _mamba2(u, W_in, b_in, A_log, D_skip, dt_bias, W_out, b_out):
            B, L, _ = u.shape
            zxbcdt = u @ W_in + b_in
            z = zxbcdt[..., :INNER]
            xs = zxbcdt[..., INNER:2 * INNER].reshape(B, L, HEADS, HEAD_DIM)
            Bm = zxbcdt[..., 2 * INNER:2 * INNER + STATE]
            Cm = zxbcdt[..., 2 * INNER + STATE:2 * INNER + 2 * STATE]
            dt = jax.nn.softplus(zxbcdt[..., 2 * INNER + 2 * STATE:] + dt_bias)
            A = -jnp.exp(A_log)
            decay = jnp.exp(dt * A)
            dtx = dt[..., None] * xs

            def step(h, inp):
                dec_t, dtx_t, B_t, C_t = inp
                h = dec_t[:, :, None, None] * h + dtx_t[..., None] * B_t[:, None, None, :]
                y = jnp.einsum('bhpn,bn->bhp', h, C_t)
                return (h, y)
            h0 = jnp.zeros((B, HEADS, HEAD_DIM, STATE), u.dtype)
            scan_in = (jnp.moveaxis(decay, 1, 0), jnp.moveaxis(dtx, 1, 0), jnp.moveaxis(Bm, 1, 0), jnp.moveaxis(Cm, 1, 0))
            _, ys = jax.lax.scan(step, h0, scan_in)
            y = jnp.moveaxis(ys, 0, 1)
            y = y + D_skip[None, None, :, None] * xs
            y = y.reshape(B, L, INNER) * jax.nn.silu(z)
            return y @ W_out + b_out
        normed = _layer_norm(input_tensor, ln_gamma, ln_beta)
        out = _mamba2(normed, W_in, b_in, A_log, D_skip, dt_bias, W_out, b_out)
        return input_tensor + out

    def _L0_ffn_ref(x, W_r, W_k, W_v, mu_r, mu_k):
        import jax, jax.numpy as jnp
        import numpy as np
        DIM = 128

        def _reference_tuple_inner(x, W_r, W_k, W_v, mu_r, mu_k):
            B, T, C = x.shape
            x_prev = jnp.concatenate([jnp.zeros((B, 1, C), x.dtype), x[:, :-1, :]], axis=1)
            xr = mu_r * x + (1.0 - mu_r) * x_prev
            xk = mu_k * x + (1.0 - mu_k) * x_prev
            r = jax.nn.sigmoid(jnp.einsum('btc,dc->btd', xr, W_r))
            k = jnp.einsum('btc,dc->btd', xk, W_k)
            k_act = jnp.square(jax.nn.relu(k))
            out = r * jnp.einsum('btc,dc->btd', k_act, W_v)
            new_state = x[:, -1, :]
            return (out, new_state)
        return _reference_tuple_inner(x, W_r, W_k, W_v, mu_r, mu_k)[0]
    x = L0_attn_input_tensor
    xn = _layernorm(x, axis=-1)
    s = _L0_attn_ref(xn, L0_attn_ln_gamma, L0_attn_ln_beta, L0_attn_W_in, L0_attn_b_in, L0_attn_A_log, L0_attn_D_skip, L0_attn_dt_bias, L0_attn_W_out, L0_attn_b_out)
    g = _silu(_L0_ffn_ref(xn, L0_ffn_W_r, L0_ffn_W_k, L0_ffn_W_v, L0_ffn_mu_r, L0_ffn_mu_k))
    x = x + s * g
    return x

_drawn_inputs = setup_inputs


def setup_inputs(seed=0):
    import zlib

    import numpy as np

    out = dict(_drawn_inputs(seed))
    spreads = {'L0_attn_ln_gamma': (1.0, 0.6),
     'L0_attn_ln_beta': (0.0, 0.8),
     'L0_attn_b_in': (0.0, 0.8),
     'L0_attn_D_skip': (1.0, 0.6),
     'L0_attn_b_out': (0.0, 0.8)}
    factors = {'L0_attn_W_in': 8.0,
     'L0_attn_A_log': 8.0,
     'L0_attn_dt_bias': 8.0,
     'L0_attn_W_out': 8.0,
     'L0_ffn_W_r': 6.275,
     'L0_ffn_mu_r': 8.0}
    for name, (base, spread) in spreads.items():
        noise = np.random.default_rng([zlib.crc32(name.encode()), seed]).standard_normal(out[name].shape)
        drawn = base * np.exp(spread * noise) if base else spread * noise
        out[name] = jnp.asarray(drawn.astype(out[name].dtype))
    for name, factor in factors.items():
        out[name] = (out[name] * factor).astype(out[name].dtype)
    return out
```

```python
from contextlib import ExitStack

import numpy as np

import concourse.bass as bass
from concourse import mybir

P = 128
F32 = mybir.dt.float32
BF16 = mybir.dt.bfloat16
ALU = mybir.AluOpType
ACT = mybir.ActivationFunctionType

BATCH, SEQ, D = 32, 256, 128
HEADS, HEAD_DIM, STATE = 8, 32, 64
INNER = HEADS * HEAD_DIM
TILES = 4
SEQS = TILES * P // SEQ
GROUPS = BATCH * SEQ // (TILES * P)
TOK = TILES * P
XD = INNER + HEADS
EPS = 1e-5
LOG1P_DEG = 9
SLOTS = 4
POOL_HEADS = (1, 3, 5)
DVE_HEADS = tuple(h for h in range(HEADS) if h not in POOL_HEADS)
HALVES = INNER // P

C_GAMMA, C_BETA, C_MUR, C_MUK, C_BZ, C_BBC, C_BXS, C_DSK, C_RESET = 0, 1, 2, 3, 4, 6, 7, 9, 11
NCOL = 12
R_BXD, R_DTB, R_ALOG, R_BOUT, R_DROW = 0, XD, XD + HEADS, XD + 2 * HEADS, XD + 2 * HEADS + D
NROW = XD + 3 * HEADS + D
W_Z, W_XD, W_BC, W_K, W_R, W_V, W_O = 0, INNER, INNER + XD, INNER + XD + P, INNER + XD + 2 * P, INNER + XD + 3 * P, INNER + XD + 4 * P
NW = W_O + HALVES * D


def log1p_coefficients():
    n = LOG1P_DEG + 1
    x = 0.5 + 0.5 * np.cos((np.arange(n) + 0.5) * np.pi / n)
    return [float(c) for c in np.polynomial.Polynomial.fit(x, np.log1p(x) / x, LOG1P_DEG, domain=[0, 1], window=[0, 1]).coef]


def build(nc, x, weights, cols, rows, f32_consts, bf16_consts, out):
    coef = log1p_coefficients()
    x_tiles = x.rearrange("(n p) d -> p n d", p=P)
    out_tiles = out.rearrange("(n p) d -> p n d", p=P)

    with ExitStack() as ctx:
        def sb(name, shape, dt=F32):
            return ctx.enter_context(nc.sbuf_tensor(name, shape, dt))

        def sem(name):
            return ctx.enter_context(nc.semaphore(name))

        def pair(name, shape, dt=F32):
            return [sb(f"{name}{i}", shape, dt) for i in range(2)]

        wraw = sb("wraw", [P, NW])
        colc = sb("colc", [P, NCOL])
        rowc = sb("rowc", [P, NROW])
        fc = sb("fc", [P, TOK + P])
        eye4 = fc[:, 0:TOK]
        eye = fc[:, 0:P]
        causal = fc[:, TOK:TOK + P]
        bc = sb("bc", [P, 3 * P + HEADS * P + HALVES * P], BF16)
        eye_b = bc[:, 0:P]
        upto_b = bc[:, P:2 * P]
        after_b = bc[:, 2 * P:3 * P]
        sel_head = bc[0:24, 3 * P:3 * P + HEADS * P].rearrange("k (h m) -> k h m", h=HEADS)
        sel_half = bc[0:24, 3 * P + HEADS * P:].rearrange("k (c m) -> k c m", c=HALVES)
        w_in = sb("w_in", [P, W_K])
        w_skip = sb("w_skip", [P, INNER])
        w_out = sb("w_out", [P, HALVES * D])
        bias_col = sb("bias_col", [P, 5])
        half_bias = sb("half_bias", [P, 2])
        bias_xd = sb("bias_xd", [P, XD])
        neg_a = sb("neg_a", [P, HEADS])

        x_all = sb("x_all", [P, GROUPS * TILES, D])
        stats = sb("stats", [P, TILES, 6])
        mean, m_gap, m_gap2, q_sum, q_all = (sb(n, [P, TILES]) for n in ("mean", "m_gap", "m_gap2", "q_sum", "q_all"))
        variances = sb("variances", [P, 2, TILES])
        minus_half = sb("minus_half", [P, 2, TILES])
        rstd = sb("rstd", [P, 2, TILES])
        xc = sb("xc", [P, TILES, D])
        xn = sb("xn", [P, TILES, D])
        uh = sb("uh", [P, TILES, D])
        xn_bias = pair("xn_bias", [P, TILES, D])
        xn_t = sb("xn_t", [P, SEQS, SEQ + 1])
        u_t = pair("u_t", [P, TOK])
        diff = sb("diff", [P, SEQS, SEQ])
        xr_t = sb("xr_t", [P, SEQS, SEQ])
        xk_t = sb("xk_t", [P, SEQS, SEQ])
        k_relu = sb("k_relu", [P, TOK])
        k_act = sb("k_act", [P, TOK])
        z_t = sb("z_t", [P, HALVES, TOK])
        z_tanh = sb("z_tanh", [P, HALVES, TOK])
        z_silu2 = pair("z_silu2", [P, HALVES, TOK])
        b_t = sb("b_t", [STATE, TOK])
        c_t = sb("c_t", [STATE, TOK])
        xs_dt = sb("xs_dt", [P, TILES, XD])
        dt_abs = sb("dt_abs", [P, TILES, HEADS])
        dt_exp = sb("dt_exp", [P, TILES, HEADS])
        poly = sb("poly", [P, 2, TILES, HEADS])
        dt = sb("dt", [P, TILES, HEADS])
        dt_a = sb("dt_a", [P, TILES, HEADS])
        dt_a_rest = sb("dt_a_rest", [P, TILES, HEADS])
        dt_a_parts = sb("dt_a_parts", [P, 3, TILES, HEADS], BF16)
        decays = sb("decays", [P, 4 + 2 * SEQS, HEADS])
        decays_rest = sb("decays_rest", [P, 4 + SEQS, HEADS])
        decay_parts = sb("decay_parts", [P, 4 + SEQS, 32], BF16)
        zeros = sb("zeros", [P, 4 + SEQS, HEADS])
        decay_rows = pair("decay_rows", [32, (4 + SEQS) * P], BF16)
        dtx = pair("dtx", [P, TILES, INNER])
        dtx_r = pair("dtx_r", [P, SEQS, INNER])
        g_diag = pair("g_diag", [P, TILES, P])
        g_off = pair("g_off", [P, SEQS, P])
        masks = sb("masks", [P, SLOTS, TOK])
        p_bc = sb("p_bc", [P, HALVES, SEQS, P])
        y_off = sb("y_off", [P, HALVES, SEQS, P])
        y_sum = sb("y_sum", [P, HALVES, SEQS, P])
        yz = sb("yz", [P, HALVES, TOK])
        r_tanh = sb("r_tanh", [P, TOK])
        rkv = sb("rkv", [P, TOK])
        rkv_tanh = sb("rkv_tanh", [P, TOK])
        gate4 = pair("gate4", [P, TOK])
        s_out = sb("s_out", [P, TOK])
        s_gate = sb("s_gate", [P, TOK])

        front = [ctx.enter_context(nc.psum_tensor(f"front{i}", [P, 512], F32)) for i in range(3)]
        bcast = [ctx.enter_context(nc.psum_tensor(f"bcast{i}", [P, 512], F32)) for i in range(2)]
        y_ps = [ctx.enter_context(nc.psum_tensor(f"y_ps{i}", [P, 512], F32)) for i in range(2)]
        misc = ctx.enter_context(nc.psum_tensor("misc", [P, 512], F32))
        rows_ps = front[2][0:32, 0:(4 + SEQS) * P // 2].bitcast(BF16)

        x_in = [sem("x_in0"), sem("x_in1")]
        consts_in = sem("consts_in")
        stored = sem("stored")
        setup_pe, setup_dve, setup_act, setup_pool = sem("setup_pe"), sem("setup_dve"), sem("setup_act"), sem("setup_pool")
        norm_chain = sem("norm_chain")
        var_ready = sem("var_ready")
        xc_ready = sem("xc_ready")
        xn_ready = sem("xn_ready")
        xn_bias_ready = sem("xn_bias_ready")
        xnt_ps, ut_ps = sem("xnt_ps"), sem("ut_ps")
        xnt_ready, ut_ready = sem("xnt_ready"), sem("ut_ready")
        diff_ready = sem("diff_ready")
        xr_ready, xk_ready = sem("xr_ready"), sem("xk_ready")
        xs_ps = sem("xs_ps")
        xs_taken = sem("xs_taken")
        z_ps = sem("z_ps")
        z_taken = sem("z_taken")
        z_done = sem("z_done")
        bc_ps = sem("bc_ps")
        bc_ready = sem("bc_ready")
        k_ps = sem("k_ps")
        k_relu_ready, k_act_ready = sem("k_relu_ready"), sem("k_act_ready")
        g_ps = sem("g_ps")
        g_diag_ready = sem("g_diag_ready")
        g_off_ready = sem("g_off_ready")
        dt_abs_ready, dt_exp_ready = sem("dt_abs_ready"), sem("dt_exp_ready")
        dt_chain = sem("dt_chain")
        dt_ready, dt_a_ready = sem("dt_ready"), sem("dt_a_ready")
        dt_parts_ready = sem("dt_parts_ready")
        sums_ps = sem("sums_ps")
        decays_ready = sem("decays_ready")
        split_chain = sem("split_chain")
        parts_ready = sem("parts_ready")
        rows_done = sem("rows_done")
        rows_ready = sem("rows_ready")
        dtx_ready, dtx_r_ready = sem("dtx_ready"), sem("dtx_r_ready")
        r_ps, v_ps = sem("r_ps"), sem("v_ps")
        r_tanh_ready, rkv_ready, rkv_tanh_ready, gate4_ready = sem("r_tanh_ready"), sem("rkv_ready"), sem("rkv_tanh_ready"), sem("gate4_ready")
        skip_done = sem("skip_done")
        bcast_ps = sem("bcast_ps")
        scan_done = sem("scan_done")
        mask_dve = sem("mask_dve")
        mask_pool = sem("mask_pool")
        y_done = sem("y_done")
        p_ps, p_ready = sem("p_ps"), sem("p_ready")
        off_ps, off_ready = sem("off_ps"), sem("off_ready")
        y_chain = sem("y_chain")
        yz_ready = sem("yz_ready")
        out_ps = sem("out_ps")
        s_ready, s_gate_ready, final_ready = sem("s_ready"), sem("s_gate_ready"), sem("final_ready")

        def after(eng, semaphore, value):
            if not isinstance(value, int) or value > 0:
                eng.wait_ge(semaphore, value)

        def steps(eng, body):
            for s in range(3):
                body(s, s % 2)
            with eng.Fori(1, (GROUPS - 2) // 2) as k:
                body(k * 2 + 1, 1, True)
                body(k * 2 + 2, 0, True)
            for s in range(GROUPS - 1, GROUPS + 2):
                body(s, s % 2)

        block = ctx.enter_context(nc.Block())

        @block.sync
        def _(sp):
            sp.dma_start(x_all[:, 0:TILES, :], x_tiles[:, 0:TILES, :]).then_inc(x_in[0], 16)
            sp.dma_start(colc[:, :], cols).then_inc(consts_in, 16)
            sp.dma_start(wraw[:, :], weights).then_inc(consts_in, 16)
            sp.dma_start(rowc[:, :], rows).then_inc(consts_in, 16)
            sp.dma_start(fc[:, :], f32_consts).then_inc(consts_in, 16)
            sp.dma_start(bc[:, :], bf16_consts).then_inc(consts_in, 16)
            sp.dma_start(x_all[:, TILES:2 * TILES, :], x_tiles[:, TILES:2 * TILES, :]).then_inc(x_in[1], 16)
            with sp.Fori(1, GROUPS // 2) as k:
                for i in range(2):
                    sp.wait_ge(x_in[i], k * 16)
                    at = bass.ds((k * 2 + i) * TILES, TILES)
                    sp.dma_start(x_all[:, at, :], x_tiles[:, at, :]).then_inc(x_in[i], 16)
            with sp.Fori(0, GROUPS, 1) as g:
                sp.wait_ge(final_ready, g + 1)
                at = bass.ds(g * TILES, TILES)
                sp.dma_start(out_tiles[:, at, :], x_all[:, at, :]).then_inc(stored, 16)
            sp.wait_ge(stored, 16 * GROUPS)

        @block.tensor
        def _(pe):
            mm = nc.tensor.matmul

            pe.wait_ge(consts_in, 80)
            beta = colc[:, C_BETA:C_BETA + 1]
            for n, at in enumerate((W_Z, W_Z + P, W_BC, W_XD, W_XD + P)):
                mm(misc[:, n:n + 1], wraw[:, at:at + P], beta, start=True, stop=True)
            pe.wait_ge(setup_dve, 1)
            mm(misc[:, P:P + XD], xc[:, 0, :], wraw[:, W_XD:W_XD + XD], start=True, stop=True).then_inc(setup_pe, 1)
            pe.wait_ge(setup_dve, 2)
            pe.wait_ge(setup_act, 1)

            def spread(b, p, h):
                after(pe, scan_done, b * 8 + (h - 1))
                mm(bcast[h % 2][:, :], sel_head[:, h, :], decay_rows[p][0:24, 0:TOK],
                   start=True, stop=True).then_inc(bcast_ps, 1)

            def project_xs(p, t):
                mm(front[(2 + t) % 3][:, 0:XD], u_t[p][:, t * P:(t + 1) * P], w_in[:, W_XD:W_XD + XD],
                   start=True, stop=True).then_inc(xs_ps, 1)

            def apply_mask(b, p, h):
                if h in POOL_HEADS:
                    pe.wait_ge(mask_pool, b * len(POOL_HEADS) + (POOL_HEADS.index(h) + 1))
                else:
                    pe.wait_ge(mask_dve, b * len(DVE_HEADS) + (DVE_HEADS.index(h) + 1))
                q = 32 * (h % 4)
                for t in range(TILES):
                    last = mm(y_ps[h // 4][q:q + 32, t * P:(t + 1) * P], dtx[p][:, t, h * HEAD_DIM:(h + 1) * HEAD_DIM],
                              masks[:, h % SLOTS, t * P:(t + 1) * P], start=False, stop=True, skip_group_check=True)
                last.then_inc(y_done, 1)

            def step(s, p, full=False):
                f, b, o = (True, True, True) if full else (s < GROUPS, 1 <= s <= GROUPS, s >= 2)
                g, gb, go, pb = s, s - 1, s - 2, 1 - p
                if f:
                    pe.wait_ge(xn_ready, g * 8 + 8)
                    after(pe, r_tanh_ready, g)
                    for t in range(TILES):
                        last = nc.tensor.transpose(front[1][:, t * P:(t + 1) * P], uh[:, t, :], eye)
                    last.then_inc(ut_ps, 1)
                    after(pe, decays_ready, g * 2)
                    for t in range(TILES):
                        last = nc.tensor.transpose(front[0][:, t * P:(t + 1) * P], xn[:, t, :], eye)
                    last.then_inc(xnt_ps, 1)
                if b:
                    pe.wait_ge(rows_ready, gb + 1)
                    spread(gb, pb, 0)
                    spread(gb, pb, 1)
                if f:
                    pe.wait_ge(ut_ready, g + 1)
                    after(pe, rows_ready, g)
                    project_xs(p, 0)
                    pe.wait_ge(xnt_ready, g + 1)
                    project_xs(p, 1)
                if b:
                    spread(gb, pb, 2)
                if f:
                    project_xs(p, 2)
                    pe.wait_ge(xs_taken, g * 4 + 1)
                    project_xs(p, 3)
                if b:
                    spread(gb, pb, 3)
                    after(pe, yz_ready, gb * 4)
                    for c in range(HALVES):
                        last = mm(y_ps[c][:, :], w_skip[:, c * P:(c + 1) * P], u_t[pb][:, :], start=True, stop=True,
                                  skip_group_check=True)
                    last.then_inc(skip_done, 1)
                    pe.wait_ge(dtx_ready, gb + 1)
                    apply_mask(gb, pb, 0)
                if f:
                    for c in range(HALVES):
                        pe.wait_ge(xs_taken, g * 4 + 2 + c)
                        mm(front[c][:, :], w_in[:, W_Z + c * P:W_Z + (c + 1) * P], u_t[p][:, :],
                           start=True, stop=True).then_inc(z_ps, 1)
                if b:
                    spread(gb, pb, 4)
                    apply_mask(gb, pb, 1)
                if f:
                    pe.wait_ge(xs_taken, g * 4 + 4)
                    mm(front[2][:, :], w_in[:, W_BC:W_BC + P], u_t[p][:, :], start=True, stop=True).then_inc(bc_ps, 1)
                if b:
                    apply_mask(gb, pb, 2)
                    spread(gb, pb, 5)
                if o:
                    pe.wait_ge(yz_ready, go * 4 + 4)
                    pe.wait_ge(rkv_ready, s if full else min(s, GROUPS))
                    for t in range(TILES):
                        for c in range(HALVES):
                            last = mm(misc[:, t * P:(t + 1) * P], yz[:, c, t * P:(t + 1) * P], w_out[:, c * D:(c + 1) * D],
                                      start=(c == 0), stop=(c == HALVES - 1))
                    last.then_inc(out_ps, 1)
                if f:
                    pe.wait_ge(z_taken, g * 4 + 2)
                    pe.wait_ge(xk_ready, g + 1)
                    mm(front[0][:, :], wraw[:, W_K:W_K + P], xk_t[:, :, :], start=True, stop=True).then_inc(k_ps, 1)
                if f:
                    pe.wait_ge(z_taken, g * 4 + 4)
                    pe.wait_ge(bc_ready, g * 2 + 2)
                    for q in range(SEQS):
                        a = q * SEQ
                        mm(front[1 + q][:, 0:SEQ], b_t[:, a:a + P], c_t[:, a:a + SEQ], start=True, stop=True)
                        mm(front[1 + q][:, SEQ:SEQ + P], b_t[:, a + P:a + SEQ], c_t[:, a + P:a + SEQ],
                           start=True, stop=True).then_inc(g_ps, 1)
                if b:
                    if o:
                        pe.wait_ge(s_ready, go + 1)
                    for c in range(HALVES):
                        last = mm(misc[:, c * 2 * P:(c + 1) * 2 * P], sel_half[:, c, :], decay_rows[pb][0:24, TOK:TOK + SEQS * P],
                                  start=True, stop=True)
                    last.then_inc(p_ps, 1)
                    spread(gb, pb, 6)
                    apply_mask(gb, pb, 3)
                if f:
                    pe.wait_ge(k_relu_ready, g + 1)
                    pe.wait_ge(dt_parts_ready, g + 1)
                    for n, (mask, t0) in enumerate(((upto_b, 1), (after_b, 0))):
                        for part in range(3):
                            last = mm(front[0][:, n * 16:n * 16 + 16], mask, dt_a_parts[:, part, t0:TILES:2, :],
                                      start=(part == 0), stop=(part == 2))
                    last.then_inc(sums_ps, 1)
                if b:
                    pe.wait_ge(p_ready, gb + 1)
                    pe.wait_ge(dtx_r_ready, gb + 1)
                    pe.wait_ge(g_off_ready, gb * 2 + 2)
                    for c in range(HALVES):
                        for q in range(SEQS):
                            last = mm(misc[:, (c * SEQS + q) * P:(c * SEQS + q + 1) * P], dtx_r[pb][:, q, c * P:(c + 1) * P],
                                      g_off[pb][:, q, :], start=True, stop=True)
                    last.then_inc(off_ps, 1)
                if f:
                    pe.wait_ge(xr_ready, g + 1)
                    pe.wait_ge(g_diag_ready, g * 2 + 1)
                    pe.wait_ge(g_off_ready, g * 2 + 1)
                    for t in range(TILES):
                        last = mm(front[1][:, t * P:(t + 1) * P], xr_t[:, t // 2, (t % 2) * P:(t % 2 + 1) * P],
                                  wraw[:, W_R:W_R + P], start=True, stop=True)
                    last.then_inc(r_ps, 1)
                if b:
                    spread(gb, pb, 7)
                    apply_mask(gb, pb, 4)
                if f:
                    pe.wait_ge(g_diag_ready, g * 2 + 2)
                    pe.wait_ge(g_off_ready, g * 2 + 2)
                    pe.wait_ge(parts_ready, g + 1)
                    for t in range(TILES + SEQS):
                        last = nc.tensor.transpose(rows_ps[:, t * P:(t + 1) * P], decay_parts[:, t, :], eye_b)
                    last.then_inc(rows_done, 1)
                if b:
                    apply_mask(gb, pb, 5)
                if f:
                    if b:
                        pe.wait_ge(off_ready, gb + 1)
                    pe.wait_ge(k_act_ready, g + 1)
                    for t in range(TILES):
                        last = mm(misc[:, t * P:(t + 1) * P], k_act[:, t * P:(t + 1) * P], wraw[:, W_V:W_V + P],
                                  start=True, stop=True)
                    last.then_inc(v_ps, 1)
                if b:
                    apply_mask(gb, pb, 6)
                    apply_mask(gb, pb, 7)

            steps(pe, step)

        @block.scalar
        def _(act):
            fn = nc.scalar.activation
            act.wait_ge(consts_in, 80)
            fn(neg_a[:, :], rowc[:, R_ALOG:R_ALOG + HEADS], ACT.Exp).then_inc(setup_act, 1)

            act.wait_ge(setup_dve, 2)

            def normalise(g):
                act.wait_ge(xc_ready, g * 2 + 2)
                after(act, xnt_ps, g)
                after(act, ut_ps, g)
                after(act, xn_bias_ready, g)
                for kind, dst in ((1, uh), (0, xn)):
                    for t in range(TILES):
                        fn(dst[:, t, :], xc[:, t, :], ACT.Copy, scale=rstd[:, kind, t:t + 1]).then_inc(xn_ready, 1)

            normalise(0)

            def step(s, p, full=False):
                n, f, b = (True,) * 3 if full else (s + 1 < GROUPS, s < GROUPS, 1 <= s <= GROUPS)
                g, gb = s, s - 1
                if f:
                    pe_xn = front[0][:, :].rearrange("p (q t) -> p q t", q=SEQS)
                    act.wait_ge(ut_ps, g + 1)
                    after(act, skip_done, g - 1)
                    fn(u_t[p][:, :], front[1][:, :], ACT.Copy).then_inc(ut_ready, 1)
                    act.wait_ge(xnt_ps, g + 1)
                    after(act, xk_ready, g)
                    fn(xn_t[:, :, 1:SEQ + 1], pe_xn, ACT.Copy).then_inc(xnt_ready, 1)
                    act.wait_ge(xs_taken, g * 4 + 4)
                    after(act, dt_ready, g)
                    fn(dt_abs[:, :, :], xs_dt[:, :, INNER:XD], ACT.Abs).then_inc(dt_abs_ready, 1)
                    act.wait_ge(dt_abs_ready, g + 1)
                    fn(dt_exp[:, :, :], dt_abs[:, :, :], ACT.Exp, scale=-1.0).then_inc(dt_exp_ready, 1)
                    for c in range(HALVES):
                        act.wait_ge(z_ps, g * 2 + c + 1)
                        after(act, z_done, g * 2 + c - 1)
                        fn(z_t[:, c, :], front[c][:, :], ACT.Identity, bias=bias_col[:, c:c + 1]).then_inc(z_taken, 1)
                        fn(z_tanh[:, c, :], front[c][:, :], ACT.Tanh, bias=half_bias[:, c:c + 1], scale=0.5).then_inc(z_taken, 1)
                    act.wait_ge(bc_ps, g + 1)
                    after(act, g_ps, g * 2)
                    fn(b_t[:, :], front[2][0:STATE, :], ACT.Identity, bias=bias_col[0:STATE, 2:3]).then_inc(bc_ready, 1)
                    fn(c_t[:, :], front[2][STATE:P, :], ACT.Identity, bias=bias_col[STATE:P, 2:3]).then_inc(bc_ready, 1)
                    act.wait_ge(k_ps, g + 1)
                    fn(k_relu[:, :], front[0][:, :], ACT.Relu).then_inc(k_relu_ready, 1)
                if b:
                    act.wait_ge(p_ps, gb + 1)
                    after(act, off_ready, gb)
                    fn(p_bc[:, :, :, :], misc[:, :].rearrange("p (c q t) -> p c q t", c=HALVES, q=SEQS), ACT.Copy).then_inc(p_ready, 1)
                if f:
                    act.wait_ge(k_relu_ready, g + 1)
                    after(act, v_ps, g)
                    fn(k_act[:, :], k_relu[:, :], ACT.Square).then_inc(k_act_ready, 1)
                    after(act, off_ps, g - 1)
                    for q in range(SEQS):
                        act.wait_ge(g_diag_ready, g * 2 + q + 1)
                        fn(g_off[p][:, q, :], front[1 + q][:, P:SEQ], ACT.Copy).then_inc(g_off_ready, 1)
                    act.wait_ge(dt_a_ready, g + 1)
                    after(act, parts_ready, g)
                    after(act, dtx_r_ready, g)
                    fn(decays[:, 0:TILES, :], dt_a[:, :, :], ACT.Exp, bias=colc[:, C_RESET:C_RESET + 1]).then_inc(decays_ready, 1)
                    act.wait_ge(sums_ps, g + 1)
                    fn(decays[:, TILES:TILES + 2 * SEQS, :], front[0][:, 0:32].rearrange("p (t h) -> p t h", h=HEADS),
                       ACT.Exp).then_inc(decays_ready, 1)
                    act.wait_ge(r_ps, g + 1)
                    after(act, rkv_ready, g)
                    fn(r_tanh[:, :], front[1][:, :], ACT.Tanh, scale=0.5).then_inc(r_tanh_ready, 1)
                    act.wait_ge(rows_done, g + 1)
                    after(act, bcast_ps, (g - 1) * 8)
                    after(act, p_ps, g - 1)
                    fn(decay_rows[p][:, :], rows_ps, ACT.Copy).then_inc(rows_ready, 1)
                if n:
                    normalise(g + 1)
                if f:
                    act.wait_ge(rkv_ready, g + 1)
                    after(act, gate4_ready, g)
                    fn(rkv_tanh[:, :], rkv[:, :], ACT.Tanh, scale=0.25).then_inc(rkv_tanh_ready, 1)

            steps(act, step)

        @block.gpsimd
        def _(pool):
            tt = nc.gpsimd.tensor_tensor
            nc.gpsimd.memset(xn_t[:, :, 0:1], 0.0)
            nc.gpsimd.memset(zeros[:, :, :], 0.0)
            nc.gpsimd.memset(decay_parts[:, :, 24:32], 0.0)
            nc.gpsimd.memset(minus_half[:, :, :], -0.5).then_inc(setup_pool, 1)
            pool.wait_ge(setup_pool, 1)
            pool.wait_ge(consts_in, 80)

            def per_tile(column):
                return column.unsqueeze(2).to_broadcast([P, TILES, D])

            def normalise(g):
                pool.wait_ge(var_ready, g * 2 + 2)
                at = bass.ds(g * TILES, TILES)
                after(pool, xn_ready, g * 8)
                tt(rstd[:, :, :], variances[:, :, :], minus_half[:, :, :], ALU.pow).then_inc(xc_ready, 1)
                tt(xc[:, :, :], x_all[:, at, :], per_tile(mean[:, :]), ALU.subtract).then_inc(xc_ready, 1)

            def mask_head(b, p, h):
                pool.wait_ge(scan_done, b * 8 + h + 1)
                tt(masks[:, h % SLOTS, :], masks[:, h % SLOTS, :], g_diag[p][:, :, :].rearrange("p t i -> p (t i)"),
                   ALU.mult).then_inc(mask_pool, 1)

            pool.wait_ge(setup_dve, 2)
            normalise(0)

            def step(s, p, full=False):
                n, f, b, o = (True,) * 4 if full else (s + 1 < GROUPS, s < GROUPS, 1 <= s <= GROUPS, s >= 2)
                g, gb, go, pb = s, s - 1, s - 2, 1 - p
                if f:
                    pool.wait_ge(xnt_ready, g + 1)
                    after(pool, xk_ready, g)
                    tt(diff[:, :, :], xn_t[:, :, 1:SEQ + 1], xn_t[:, :, 0:SEQ], ALU.subtract).then_inc(diff_ready, 1)
                if b:
                    mask_head(gb, pb, 1)
                if b:
                    mask_head(gb, pb, 3)
                if n:
                    normalise(g + 1)
                if o:
                    pool.wait_ge(s_ready, go + 1)
                    pool.wait_ge(gate4_ready, go + 1)
                    after(pool, final_ready, go)
                    tt(s_gate[:, :], s_out[:, :], gate4[p][:, :], ALU.mult).then_inc(s_gate_ready, 1)
                if b:
                    mask_head(gb, pb, 5)
                if f:
                    pool.wait_ge(decays_ready, g * 2 + 2)
                    after(pool, rows_done, g)
                    wide, part = decays[:, 0:TILES + SEQS, :], decay_parts
                    tt(part[:, :, 0:8], wide, zeros[:, :, :], ALU.add).then_inc(split_chain, 1)
                    pool.wait_ge(split_chain, g * 3 + 1)
                    tt(decays_rest[:, :, :], wide, part[:, :, 0:8], ALU.subtract).then_inc(split_chain, 1)
                    pool.wait_ge(split_chain, g * 3 + 2)
                    tt(part[:, :, 8:16], decays_rest[:, :, :], zeros[:, :, :], ALU.add).then_inc(split_chain, 1)
                    pool.wait_ge(split_chain, g * 3 + 3)
                    tt(part[:, :, 16:24], decays_rest[:, :, :], part[:, :, 8:16], ALU.subtract).then_inc(parts_ready, 1)
                if f:
                    pool.wait_ge(xn_ready, g * 8 + 8)
                    after(pool, s_ready, g - 1)
                    tt(xn_bias[p][:, :, :], xn[:, :, :], rowc[:, R_BOUT:R_BOUT + D].unsqueeze(1).to_broadcast([P, TILES, D]),
                       ALU.add).then_inc(xn_bias_ready, 1)
                if f:
                    pool.wait_ge(dt_ready, g + 1)
                    after(pool, y_done, (g - 1) * 8)
                    for t in range(TILES):
                        last = tt(dtx[p][:, t, :].rearrange("p (h e) -> p h e", h=HEADS),
                                  xs_dt[:, t, 0:INNER].rearrange("p (h e) -> p h e", h=HEADS),
                                  dt[:, t, :].unsqueeze(2).to_broadcast([P, HEADS, HEAD_DIM]), ALU.mult)
                    last.then_inc(dtx_ready, 1)
                if f:
                    pool.wait_ge(dtx_ready, g + 1)
                    after(pool, off_ps, g - 1)
                    for q in range(SEQS):
                        last = tt(dtx_r[p][:, q, :].rearrange("p (h e) -> p h e", h=HEADS),
                                  dtx[p][:, 2 * q, :].rearrange("p (h e) -> p h e", h=HEADS),
                                  decays[:, TILES + SEQS + q, :].unsqueeze(2).to_broadcast([P, HEADS, HEAD_DIM]), ALU.mult)
                    last.then_inc(dtx_r_ready, 1)

            steps(pool, step)

        @block.vector
        def _(dve):
            v = nc.vector
            dve.wait_ge(consts_in, 80)
            v.tensor_copy(xc[:, 0, :], colc[:, C_BETA:C_BETA + 1].to_broadcast([P, P])).then_inc(setup_dve, 1)
            v.tensor_scalar(w_in[:, :], wraw[:, 0:W_K], colc[:, C_GAMMA:C_GAMMA + 1], None, ALU.mult).then_inc(dt_chain, 1)
            v.tensor_scalar(w_out[:, :], wraw[:, W_O:W_O + HALVES * D], 0.5, None, ALU.mult)
            dve.wait_ge(dt_chain, 1)
            v.tensor_tensor(w_skip[:, :].rearrange("p (h e) -> p h e", h=HEADS),
                            w_in[:, W_XD:W_XD + INNER].rearrange("p (h e) -> p h e", h=HEADS),
                            rowc[:, R_DROW:R_DROW + HEADS].unsqueeze(2).to_broadcast([P, HEADS, HEAD_DIM]), ALU.mult)
            dve.wait_ge(setup_pe, 1)
            v.tensor_tensor(bias_col[:, :], misc[:, 0:5], colc[:, C_BZ:C_BZ + 5], ALU.add).then_inc(dt_chain, 1)
            v.tensor_tensor(bias_xd[:, :], misc[:, P:P + XD], rowc[:, R_BXD:R_BXD + XD], ALU.add).then_inc(dt_chain, 1)
            dve.wait_ge(dt_chain, 3)
            v.tensor_scalar(half_bias[:, :], bias_col[:, 0:2], 0.5, None, ALU.mult)
            v.tensor_tensor(bias_col[:, 3:5], bias_col[:, 3:5], colc[:, C_DSK:C_DSK + 2], ALU.mult)
            v.tensor_tensor(bias_xd[:, INNER:XD], bias_xd[:, INNER:XD], rowc[:, R_DTB:R_DTB + HEADS], ALU.add)
            dve.wait_ge(setup_act, 1)
            v.tensor_scalar(neg_a[:, :], neg_a[:, :], -1.0, None, ALU.mult).then_inc(setup_dve, 1)
            dve.wait_ge(setup_dve, 2)

            SETUP = 3

            def norm_stats(g, i, t):
                if t == 0:
                    dve.wait_ge(x_in[i], g * 8 + (16 - 8 * i))
                    after(dve, norm_chain, g * 9)
                v.bn_stats(stats[:, t, :], x_all[:, bass.ds(g * TILES + t, 1), :].rearrange("p o d -> p (o d)")).then_inc(norm_chain, 1)

            m_even, q_even, m_odd, q_odd = (stats[:, :, k] for k in (1, 2, 4, 5))

            def norm_gaps(g):
                dve.wait_ge(norm_chain, g * 9 + 4)
                v.tensor_tensor(m_gap[:, :], m_even, m_odd, ALU.subtract).then_inc(norm_chain, 1)
                v.tensor_tensor(q_sum[:, :], q_even, q_odd, ALU.add).then_inc(norm_chain, 1)

            def norm_mean(g):
                dve.wait_ge(norm_chain, g * 9 + 6)
                after(dve, xc_ready, g * 2)
                v.scalar_tensor_tensor(out=mean[:, :], in0=m_gap[:, :], scalar=-0.5, in1=m_even,
                                       op0=ALU.mult, op1=ALU.add).then_inc(norm_chain, 1)
                v.tensor_tensor(m_gap2[:, :], m_gap[:, :], m_gap[:, :], ALU.mult).then_inc(norm_chain, 1)

            def norm_deviations(g):
                dve.wait_ge(norm_chain, g * 9 + 8)
                v.scalar_tensor_tensor(out=q_all[:, :], in0=m_gap2[:, :], scalar=D / 4.0, in1=q_sum[:, :],
                                       op0=ALU.mult, op1=ALU.add).then_inc(norm_chain, 1)

            def norm_variances(g):
                dve.wait_ge(norm_chain, g * 9 + 9)
                v.tensor_scalar(variances[:, 0, :], q_all[:, :], 1.0 / D, EPS, ALU.mult, ALU.add).then_inc(var_ready, 1)
                v.tensor_scalar(variances[:, 1, :], q_all[:, :], (1.0 + EPS) / D, EPS * EPS, ALU.mult, ALU.add).then_inc(var_ready, 1)

            def scan(b, h):
                dve.wait_ge(bcast_ps, b * 8 + h + 1)
                after(dve, y_done, b * 8 + (h + 1 - SLOTS))
                v.tensor_tensor_scan(masks[:, h % SLOTS, :], bcast[h % 2][:, :], eye4, 0.0, ALU.mult, ALU.add).then_inc(scan_done, 1)

            def mask_head(b, p, h):
                dve.wait_ge(scan_done, b * 8 + h + 1)
                v.tensor_tensor(masks[:, h % SLOTS, :], masks[:, h % SLOTS, :],
                                g_diag[p][:, :, :].rearrange("p t i -> p (t i)"), ALU.mult).then_inc(mask_dve, 1)

            def take_xs(g, t):
                dve.wait_ge(xs_ps, g * 4 + t + 1)
                if t == 0:
                    after(dve, dtx_ready, g)
                v.tensor_tensor(xs_dt[:, t, :], front[(2 + t) % 3][:, 0:XD], bias_xd[:, :], ALU.add).then_inc(xs_taken, 1)

            def log1p(g, k):
                done = LOG1P_DEG - k
                q, e = poly[:, k % 2, :, :], dt_exp[:, :, :]
                if k == LOG1P_DEG:
                    dve.wait_ge(dt_exp_ready, g + 1)
                    v.tensor_scalar(q, e, coef[k], None, ALU.mult).then_inc(dt_chain, 1)
                else:
                    dve.wait_ge(dt_chain, g * 13 + (SETUP + done))
                    v.scalar_tensor_tensor(out=q, in0=poly[:, (k + 1) % 2, :, :], scalar=coef[k], in1=e,
                                           op0=ALU.add, op1=ALU.mult).then_inc(dt_chain, 1)

            def dt_value(g):
                dve.wait_ge(dt_chain, g * 13 + (SETUP + 10))
                v.scalar_tensor_tensor(out=dt[:, :, :], in0=xs_dt[:, :, INNER:XD], scalar=0.0, in1=poly[:, 0, :, :],
                                       op0=ALU.max, op1=ALU.add).then_inc(dt_ready, 1)

            def dt_decay(g):
                dve.wait_ge(dt_ready, g + 1)
                after(dve, decays_ready, g * 2)
                v.tensor_tensor(dt_a[:, :, :], dt[:, :, :], neg_a[:, :].unsqueeze(1).to_broadcast([P, TILES, HEADS]),
                                ALU.mult).then_inc(dt_a_ready, 1)

            def dt_part(g, n):
                part, rest = dt_a_parts, dt_a_rest[:, :, :]
                if n == 0:
                    dve.wait_ge(dt_a_ready, g + 1)
                    after(dve, sums_ps, g)
                    v.tensor_copy(part[:, 0, :, :], dt_a[:, :, :]).then_inc(dt_chain, 1)
                else:
                    dve.wait_ge(dt_chain, g * 13 + (SETUP + 10 + n))
                if n == 1:
                    v.tensor_tensor(rest, dt_a[:, :, :], part[:, 0, :, :], ALU.subtract).then_inc(dt_chain, 1)
                if n == 2:
                    v.tensor_copy(part[:, 1, :, :], rest).then_inc(dt_chain, 1)
                if n == 3:
                    v.tensor_tensor(part[:, 2, :, :], rest, part[:, 1, :, :], ALU.subtract).then_inc(dt_parts_ready, 1)

            def take_g(g, p, q):
                dve.wait_ge(g_ps, g * 2 + q + 1)
                if q == 0:
                    after(dve, mask_pool, (g - 1) * len(POOL_HEADS))
                diagonal = front[1 + q][:, :].rearrange("p (t i) -> p t i", i=SEQ)[:, :, 0:P]
                v.tensor_tensor(g_diag[p][:, 2 * q:2 * q + 2, :], diagonal, causal.unsqueeze(1).to_broadcast([P, 2, P]),
                                ALU.mult).then_inc(g_diag_ready, 1)

            def silu_z(g, p, c):
                dve.wait_ge(z_taken, g * 4 + 2 * c + 2)
                v.scalar_tensor_tensor(out=z_silu2[p][:, c, :], in0=z_tanh[:, c, :], scalar=1.0, in1=z_t[:, c, :],
                                       op0=ALU.add, op1=ALU.mult).then_inc(z_done, 1)

            def mix(g, mu, dst, done, used):
                dve.wait_ge(diff_ready, g + 1)
                after(dve, used, g)
                v.scalar_tensor_tensor(out=dst[:, :, :], in0=diff[:, :, :], scalar=colc[:, mu:mu + 1], in1=xn_t[:, :, 0:SEQ],
                                       op0=ALU.mult, op1=ALU.add).then_inc(done, 1)

            def read_y(b, p):
                dve.wait_ge(y_done, b * 8 + 8)
                after(dve, out_ps, b)
                for c in range(HALVES):
                    y = y_ps[c][:, :].rearrange("p (q a i) -> p q a i", q=SEQS, a=2)
                    z = z_silu2[p][:, c, :].rearrange("p (q a i) -> p q a i", q=SEQS, a=2)
                    dst = yz[:, c, :].rearrange("p (q a i) -> p q a i", q=SEQS, a=2)
                    v.scalar_tensor_tensor(out=y_sum[:, c, :, :], in0=y[:, :, 1, :], scalar=bias_col[:, 3 + c:4 + c],
                                           in1=y_off[:, c, :, :], op0=ALU.add, op1=ALU.add).then_inc(y_chain, 1)
                    v.scalar_tensor_tensor(out=dst[:, :, 0, :], in0=y[:, :, 0, :], scalar=bias_col[:, 3 + c:4 + c],
                                           in1=z[:, :, 0, :], op0=ALU.add, op1=ALU.mult).then_inc(yz_ready, 1)
                    dve.wait_ge(y_chain, b * 2 + c + 1)
                    v.tensor_tensor(dst[:, :, 1, :], y_sum[:, c, :, :], z[:, :, 1, :], ALU.mult).then_inc(yz_ready, 1)

            for t in range(TILES):
                norm_stats(0, 0, t)
            norm_gaps(0)
            norm_mean(0)
            norm_deviations(0)
            norm_variances(0)

            def step(s, p, full=False):
                n, f, b, o = (True,) * 4 if full else (s + 1 < GROUPS, s < GROUPS, 1 <= s <= GROUPS, s >= 2)
                g, gb, go, pb = s, s - 1, s - 2, 1 - p
                if b:
                    scan(gb, 0)
                    mask_head(gb, pb, 0)
                    scan(gb, 1)
                if f:
                    take_xs(g, 0)
                    take_xs(g, 1)
                if b:
                    scan(gb, 2)
                if f:
                    take_xs(g, 2)
                    take_xs(g, 3)
                    mix(g, C_MUK, xk_t, xk_ready, k_ps)
                if b:
                    scan(gb, 3)
                if f:
                    log1p(g, 9)
                if n:
                    norm_stats(g + 1, 1 - p, 0)
                if f:
                    log1p(g, 8)
                if n:
                    norm_stats(g + 1, 1 - p, 1)
                if f:
                    log1p(g, 7)
                if n:
                    norm_stats(g + 1, 1 - p, 2)
                if f:
                    log1p(g, 6)
                if n:
                    norm_stats(g + 1, 1 - p, 3)
                if f:
                    log1p(g, 5)
                if b:
                    mask_head(gb, pb, 2)
                if f:
                    log1p(g, 4)
                if n:
                    norm_gaps(g + 1)
                if f:
                    log1p(g, 3)
                if n:
                    norm_mean(g + 1)
                if f:
                    log1p(g, 2)
                if n:
                    norm_deviations(g + 1)
                if f:
                    log1p(g, 1)
                if n:
                    norm_variances(g + 1)
                if f:
                    log1p(g, 0)
                if b:
                    scan(gb, 4)
                if f:
                    dt_value(g)
                    mix(g, C_MUR, xr_t, xr_ready, r_ps)
                    dt_decay(g)
                if o:
                    dve.wait_ge(out_ps, go + 1)
                    dve.wait_ge(xn_bias_ready, go + 1)
                    after(dve, s_gate_ready, go)
                    v.tensor_tensor(s_out[:, :], misc[:, :], xn_bias[p][:, :, :].rearrange("p t d -> p (t d)"),
                                    ALU.add).then_inc(s_ready, 1)
                if f:
                    dt_part(g, 0)
                    silu_z(g, p, 0)
                    dt_part(g, 1)
                if b:
                    mask_head(gb, pb, 4)
                if f:
                    dt_part(g, 2)
                    take_g(g, p, 0)
                    dt_part(g, 3)
                    take_g(g, p, 1)
                if b:
                    scan(gb, 5)
                if f:
                    silu_z(g, p, 1)
                if b:
                    scan(gb, 6)
                    mask_head(gb, pb, 6)
                    scan(gb, 7)
                    dve.wait_ge(off_ps, gb + 1)
                    dve.wait_ge(p_ready, gb + 1)
                    v.tensor_tensor(y_off[:, :, :, :].rearrange("p c q i -> p (c q i)"), misc[:, :],
                                    p_bc[:, :, :, :].rearrange("p c q i -> p (c q i)"), ALU.mult).then_inc(off_ready, 1)
                    mask_head(gb, pb, 7)
                if f:
                    dve.wait_ge(v_ps, g + 1)
                    dve.wait_ge(r_tanh_ready, g + 1)
                    after(dve, rkv_tanh_ready, g)
                    after(dve, gate4_ready, g)
                    v.scalar_tensor_tensor(out=rkv[:, :], in0=r_tanh[:, :], scalar=1.0, in1=misc[:, :],
                                           op0=ALU.add, op1=ALU.mult).then_inc(rkv_ready, 1)
                if o:
                    dve.wait_ge(s_gate_ready, go + 1)
                    at = bass.ds(go * TILES, TILES)
                    x_o = x_all[:, at, :]
                    v.scalar_tensor_tensor(out=x_o, in0=s_gate[:, :].rearrange("p (t d) -> p t d", d=D), scalar=0.25, in1=x_o,
                                           op0=ALU.mult, op1=ALU.add).then_inc(final_ready, 1)
                if b:
                    dve.wait_ge(off_ready, gb + 1)
                    read_y(gb, pb)
                if f:
                    dve.wait_ge(rkv_tanh_ready, g + 1)
                    after(dve, s_gate_ready, g - 1)
                    v.scalar_tensor_tensor(out=gate4[p][:, :], in0=rkv_tanh[:, :], scalar=1.0, in1=rkv[:, :],
                                           op0=ALU.add, op1=ALU.mult).then_inc(gate4_ready, 1)

            steps(dve, step)


def constants():
    k, m = np.indices((P, P))
    f32 = np.concatenate([np.tile(np.eye(P), (1, TILES)), k <= m], axis=1).astype(np.float32)
    row = np.arange(P)[:, None]
    real = row < 24
    head_of = np.where(real, row % HEADS, -1)
    sel_head = np.concatenate([np.repeat(head_of == h, P, axis=1) for h in range(HEADS)], axis=1)
    sel_half = head_of == (np.arange(INNER) // HEAD_DIM)[None, :]
    b16 = np.concatenate([k == m, k <= m, k > m, sel_head, sel_half], axis=1)
    return f32, b16.astype(mybir.dt.np(BF16))


def kernel(L0_attn_input_tensor, L0_attn_ln_gamma, L0_attn_ln_beta, L0_attn_W_in, L0_attn_b_in, L0_attn_A_log, L0_attn_D_skip,
           L0_attn_dt_bias, L0_attn_W_out, L0_attn_b_out, L0_ffn_W_r, L0_ffn_W_k, L0_ffn_W_v, L0_ffn_mu_r, L0_ffn_mu_k):
    import concourse.bacc as bacc
    from concourse.bass_utils import run_bass_kernel_spmd

    x = np.ascontiguousarray(np.asarray(L0_attn_input_tensor)).reshape(BATCH * SEQ, D)
    w_in, b_in = np.asarray(L0_attn_W_in), np.asarray(L0_attn_b_in)
    z, xs, bc_, dt = slice(0, INNER), slice(INNER, 2 * INNER), slice(2 * INNER, 2 * INNER + 2 * STATE), slice(2 * INNER + 2 * STATE, None)
    w_out = np.asarray(L0_attn_W_out)
    weights = np.concatenate([w_in[:, z], w_in[:, xs], w_in[:, dt], w_in[:, bc_], np.asarray(L0_ffn_W_k).T, np.asarray(L0_ffn_W_r).T,
                              np.asarray(L0_ffn_W_v).T] + [w_out[c * P:(c + 1) * P] for c in range(HALVES)], axis=1)
    reset = np.zeros(P, np.float32)
    reset[0] = -30000.0
    skip = np.repeat(np.asarray(L0_attn_D_skip), HEAD_DIM)
    cols = np.stack([np.asarray(L0_attn_ln_gamma), np.asarray(L0_attn_ln_beta), np.asarray(L0_ffn_mu_r), np.asarray(L0_ffn_mu_k),
                     b_in[0:P], b_in[P:2 * P], b_in[bc_], b_in[xs][:P], b_in[xs][P:], skip[:P], skip[P:], reset], axis=1)
    row = np.concatenate([b_in[xs], b_in[dt], np.asarray(L0_attn_dt_bias), np.asarray(L0_attn_A_log), np.asarray(L0_attn_b_out),
                          np.asarray(L0_attn_D_skip)])
    rows = np.tile(row[None, :], (P, 1))
    f32_consts, bf16_consts = constants()
    arrays = {"x": x, "weights": weights, "cols": cols, "rows": rows, "f32_consts": f32_consts, "bf16_consts": bf16_consts}
    arrays = {k: np.ascontiguousarray(a) for k, a in arrays.items()}

    nc = bacc.Bacc("TRN2", target_bir_lowering=False, num_devices=1)
    args = [nc.dram_tensor(n, list(a.shape), mybir.dt.from_np(a.dtype), kind="ExternalInput").ap() for n, a in arrays.items()]
    out = nc.dram_tensor("out", [BATCH * SEQ, D], F32, kind="ExternalOutput").ap()
    build(nc, *args, out)
    result = run_bass_kernel_spmd(nc, [arrays], core_ids=[0])
    return result.results[0]["out"].reshape(BATCH, SEQ, D)
```

```python
from contextlib import ExitStack

import numpy as np

import concourse.bass as bass
from concourse import mybir

P = 128
F32 = mybir.dt.float32
BF16 = mybir.dt.bfloat16
ALU = mybir.AluOpType
ACT = mybir.ActivationFunctionType

BATCH, SEQ, D = 32, 256, 128
HEADS, HEAD_DIM, STATE = 8, 32, 64
INNER = HEADS * HEAD_DIM
TILES = 4
SEQS = TILES * P // SEQ
GROUPS = BATCH * SEQ // (TILES * P)
TOK = TILES * P
XD = INNER + HEADS
EPS = 1e-5
LOG1P_DEG = 8
SLOTS = 4
POOL_HEADS = (1, 3, 5)
DVE_HEADS = tuple(h for h in range(HEADS) if h not in POOL_HEADS)
HALVES = INNER // P

C_GAMMA, C_BETA, C_MUR, C_MUK, C_BZ, C_BBC, C_BXS, C_DSK, C_RESET = 0, 1, 2, 3, 4, 6, 7, 9, 11
NCOL = 12
R_BXD, R_DTB, R_ALOG, R_BOUT, R_DROW = 0, XD, XD + HEADS, XD + 2 * HEADS, XD + 2 * HEADS + D
NROW = XD + 3 * HEADS + D
BIAS_ROWS = 96
W_Z, W_XD, W_BC, W_K, W_R, W_V, W_O = 0, INNER, INNER + XD, INNER + XD + P, INNER + XD + 2 * P, INNER + XD + 3 * P, INNER + XD + 4 * P
NW = W_O + HALVES * D


def log1p_coefficients():
    n = LOG1P_DEG + 1
    x = 0.5 + 0.5 * np.cos((np.arange(n) + 0.5) * np.pi / n)
    return [float(c) for c in np.polynomial.Polynomial.fit(x, np.log1p(x) / x, LOG1P_DEG, domain=[0, 1], window=[0, 1]).coef]


def build(nc, x, weights, cols, rows, f32_consts, bf16_consts, out):
    coef = log1p_coefficients()
    x_tiles = x.rearrange("(n p) d -> p n d", p=P)
    out_tiles = out.rearrange("(n p) d -> p n d", p=P)

    with ExitStack() as ctx:
        def sb(name, shape, dt=F32):
            return ctx.enter_context(nc.sbuf_tensor(name, shape, dt))

        def sem(name):
            return ctx.enter_context(nc.semaphore(name))

        def pair(name, shape, dt=F32):
            return [sb(f"{name}{i}", shape, dt) for i in range(2)]

        wraw = sb("wraw", [P, NW])
        colc = sb("colc", [P, NCOL])
        rowc = sb("rowc", [P, NROW])
        fc = sb("fc", [P, TOK])
        eye4 = fc[:, :]
        eye = fc[:, 0:P]
        bc = sb("bc", [P, 4 * P + HEADS * P + HALVES * P], BF16)
        eye_b = bc[:, 0:P]
        upto_b = bc[:, P:2 * P]
        after_b = bc[:, 2 * P:3 * P]
        sel_head = bc[0:24, 3 * P:3 * P + HEADS * P].rearrange("k (h m) -> k h m", h=HEADS)
        sel_half = bc[0:24, 3 * P + HEADS * P:3 * P + HEADS * P + INNER].rearrange("k (c m) -> k c m", c=HALVES)
        share_b = bc[0:BIAS_ROWS, 3 * P + HEADS * P + INNER:]
        w_in = sb("w_in", [P, W_K])
        w_skip = sb("w_skip", [P, INNER])
        w_v = sb("w_v", [P, D])
        row_parts = sb("row_parts", [BIAS_ROWS, XD + D], BF16)
        row_rest = sb("row_rest", [BIAS_ROWS, XD + D])
        bias_col = sb("bias_col", [P, 5])
        bias_xd = sb("bias_xd", [P, XD])
        table_warm = sb("table_warm", [P, 2])
        neg_a = sb("neg_a", [P, HEADS])

        x_all = sb("x_all", [P, GROUPS * TILES, D])
        stats = sb("stats", [P, TILES, 6])
        mean, m_gap, m_gap2, q_sum, q_all = (sb(n, [P, TILES]) for n in ("mean", "m_gap", "m_gap2", "q_sum", "q_all"))
        variances = sb("variances", [P, 2, TILES])
        minus_half = sb("minus_half", [P, 2, TILES])
        rstd = sb("rstd", [P, 2, TILES])
        xc = sb("xc", [P, TILES, D])
        xn = pair("xn", [P, TILES, D])
        uh = sb("uh", [P, TILES, D])
        xn_t = sb("xn_t", [P, SEQS, SEQ + 1])
        u_t = pair("u_t", [P, TOK])
        diff = sb("diff", [P, SEQS, SEQ])
        xr_t = sb("xr_t", [P, SEQS, SEQ])
        xk_t = sb("xk_t", [P, SEQS, SEQ])
        k_relu = sb("k_relu", [P, TOK])
        k_act = sb("k_act", [P, TOK])
        z_silu = pair("z_silu", [P, HALVES, TOK])
        b_t = sb("b_t", [STATE, TOK])
        c_t = sb("c_t", [STATE, TOK])
        xs_dt = sb("xs_dt", [P, TILES, XD])
        dt_abs = sb("dt_abs", [P, TILES, HEADS])
        dt_exp = sb("dt_exp", [P, TILES, HEADS])
        poly = sb("poly", [P, 2, TILES, HEADS])
        dt = sb("dt", [P, TILES, HEADS])
        dt_a = sb("dt_a", [P, TILES, HEADS])
        dt_a_rest = sb("dt_a_rest", [P, TILES, HEADS])
        dt_a_parts = sb("dt_a_parts", [P, 3, TILES, HEADS], BF16)
        decays = sb("decays", [P, 4 + 2 * SEQS, HEADS])
        decays_rest = sb("decays_rest", [P, 4 + SEQS, HEADS])
        decay_parts = sb("decay_parts", [P, 4 + SEQS, 32], BF16)
        zeros = sb("zeros", [P, 4 + SEQS, HEADS])
        decay_rows = pair("decay_rows", [32, (4 + SEQS) * P], BF16)
        dtx = pair("dtx", [P, TILES, INNER])
        dtx_r = pair("dtx_r", [P, SEQS, INNER])
        g_diag = pair("g_diag", [P, TILES, P])
        g_off = pair("g_off", [P, SEQS, P])
        masks = sb("masks", [P, SLOTS, TOK])
        p_bc = sb("p_bc", [P, HALVES, SEQS, P])
        y_off = sb("y_off", [P, HALVES, SEQS, P])
        y_sum = sb("y_sum", [P, HALVES, SEQS, P])
        yz = sb("yz", [P, HALVES, TOK])
        r_tanh = sb("r_tanh", [P, TOK])
        rkv = sb("rkv", [P, TOK])
        gate = pair("gate", [P, TOK])
        gated_xn = sb("gated_xn", [P, TILES, D])
        gated_out = sb("gated_out", [P, TOK])

        front = [ctx.enter_context(nc.psum_tensor(f"front{i}", [P, 512], F32)) for i in range(3)]
        bcast = [ctx.enter_context(nc.psum_tensor(f"bcast{i}", [P, 512], F32)) for i in range(2)]
        y_ps = [ctx.enter_context(nc.psum_tensor(f"y_ps{i}", [P, 512], F32)) for i in range(2)]
        misc = ctx.enter_context(nc.psum_tensor("misc", [P, 512], F32))
        rows_ps = front[0][0:32, 0:(4 + SEQS) * P // 2].bitcast(BF16)

        x_in = [sem("x_in0"), sem("x_in1")]
        consts_in = sem("consts_in")
        stored = sem("stored")
        setup_pe, setup_dve, setup_act, setup_pool = sem("setup_pe"), sem("setup_dve"), sem("setup_act"), sem("setup_pool")
        norm_chain = sem("norm_chain")
        var_ready = sem("var_ready")
        xc_ready = sem("xc_ready")
        xn_ready = sem("xn_ready")
        xnt_ps, ut_ps = sem("xnt_ps"), sem("ut_ps")
        xnt_ready, ut_ready = sem("xnt_ready"), sem("ut_ready")
        diff_ready = sem("diff_ready")
        xr_ready, xk_ready = sem("xr_ready"), sem("xk_ready")
        xs_ps = sem("xs_ps")
        xs_taken = sem("xs_taken")
        z_ps = sem("z_ps")
        z_done = sem("z_done")
        bc_ps = sem("bc_ps")
        bc_ready = sem("bc_ready")
        k_ps = sem("k_ps")
        k_relu_ready, k_act_ready = sem("k_relu_ready"), sem("k_act_ready")
        g_ps = sem("g_ps")
        g_diag_ready = sem("g_diag_ready")
        g_off_ready = sem("g_off_ready")
        dt_abs_ready, dt_exp_ready = sem("dt_abs_ready"), sem("dt_exp_ready")
        dt_chain = sem("dt_chain")
        dt_ready, dt_a_ready = sem("dt_ready"), sem("dt_a_ready")
        dt_parts_ready = sem("dt_parts_ready")
        sums_ps = sem("sums_ps")
        decays_ready = sem("decays_ready")
        split_chain = sem("split_chain")
        parts_ready = sem("parts_ready")
        rows_done = sem("rows_done")
        rows_ready = sem("rows_ready")
        dtx_ready, dtx_r_ready = sem("dtx_ready"), sem("dtx_r_ready")
        r_ps, v_ps = sem("r_ps"), sem("v_ps")
        r_tanh_ready, rkv_ready, gate_ready = sem("r_tanh_ready"), sem("rkv_ready"), sem("gate_ready")
        skip_done = sem("skip_done")
        bcast_ps = sem("bcast_ps")
        scan_done = sem("scan_done")
        mask_dve = sem("mask_dve")
        mask_pool = sem("mask_pool")
        y_done = sem("y_done")
        p_ps, p_ready = sem("p_ps"), sem("p_ready")
        off_ps, off_ready = sem("off_ps"), sem("off_ready")
        y_sum_ready = sem("y_sum_ready")
        yz_first_ready = sem("yz_first_ready")
        out_ps = sem("out_ps")
        yz_second_ready = sem("yz_second_ready")
        gated_xn_ready, residual_ready = sem("gated_xn_ready"), sem("residual_ready")
        gated_out_ready, final_ready = sem("gated_out_ready"), sem("final_ready")

        def after(eng, semaphore, value):
            if not isinstance(value, int) or value > 0:
                eng.wait_ge(semaphore, value)

        def steps(eng, body):
            for s in range(3):
                body(s, s % 2)
            with eng.Fori(1, (GROUPS - 2) // 2) as k:
                body(k * 2 + 1, 1, True)
                body(k * 2 + 2, 0, True)
            for s in range(GROUPS - 1, GROUPS + 2):
                body(s, s % 2)

        block = ctx.enter_context(nc.Block())

        @block.sync
        def _(sp):
            sp.dma_start(x_all[:, 0:TILES, :], x_tiles[:, 0:TILES, :]).then_inc(x_in[0], 16)
            sp.dma_start(colc[:, :], cols).then_inc(consts_in, 16)
            sp.dma_start(wraw[:, :], weights).then_inc(consts_in, 16)
            sp.dma_start(rowc[:, :], rows).then_inc(consts_in, 16)
            sp.dma_start(fc[:, :], f32_consts).then_inc(consts_in, 16)
            sp.dma_start(bc[:, :], bf16_consts).then_inc(consts_in, 16)
            sp.dma_start(x_all[:, TILES:2 * TILES, :], x_tiles[:, TILES:2 * TILES, :]).then_inc(x_in[1], 16)
            with sp.Fori(1, GROUPS // 2) as k:
                for i in range(2):
                    sp.wait_ge(x_in[i], k * 16)
                    at = bass.ds((k * 2 + i) * TILES, TILES)
                    sp.dma_start(x_all[:, at, :], x_tiles[:, at, :]).then_inc(x_in[i], 16)
            with sp.Fori(0, GROUPS, 1) as g:
                sp.wait_ge(final_ready, g + 1)
                at = bass.ds(g * TILES, TILES)
                sp.dma_start(out_tiles[:, at, :], x_all[:, at, :]).then_inc(stored, 16)
            sp.wait_ge(stored, 16 * GROUPS)

        @block.tensor
        def _(pe):
            mm = nc.tensor.matmul

            pe.wait_ge(consts_in, 80)
            beta = colc[:, C_BETA:C_BETA + 1]
            for n, at in enumerate((W_Z, W_Z + P, W_BC, W_XD, W_XD + P)):
                mm(misc[:, n:n + 1], wraw[:, at:at + P], beta, start=True, stop=True)
            pe.wait_ge(setup_dve, 1)
            mm(misc[:, P:P + XD], xc[:, 0, :], wraw[:, W_XD:W_XD + XD], start=True, stop=True).then_inc(setup_pe, 1)
            pe.wait_ge(setup_dve, 2)
            pe.wait_ge(setup_act, 1)

            def spread(b, p, h):
                after(pe, scan_done, b * 8 + (h - 1))
                mm(bcast[h % 2][:, :], sel_head[:, h, :], decay_rows[p][0:24, 0:TOK],
                   start=True, stop=True).then_inc(bcast_ps, 1)

            def project_xs(p, t):
                mm(front[(2 - t) % 3][:, 0:XD], share_b, row_parts[:, 0:XD], start=True, stop=False)
                mm(front[(2 - t) % 3][:, 0:XD], u_t[p][:, t * P:(t + 1) * P], w_in[:, W_XD:W_XD + XD],
                   start=False, stop=True).then_inc(xs_ps, 1)

            def apply_mask(b, p, h):
                if h in POOL_HEADS:
                    pe.wait_ge(mask_pool, b * len(POOL_HEADS) + (POOL_HEADS.index(h) + 1))
                else:
                    pe.wait_ge(mask_dve, b * len(DVE_HEADS) + (DVE_HEADS.index(h) + 1))
                q = 32 * (h % 4)
                for t in range(TILES):
                    last = mm(y_ps[h // 4][q:q + 32, t * P:(t + 1) * P], dtx[p][:, t, h * HEAD_DIM:(h + 1) * HEAD_DIM],
                              masks[:, h % SLOTS, t * P:(t + 1) * P], start=False, stop=True, skip_group_check=True)
                last.then_inc(y_done, 1)

            def transpose_inputs(g, p):
                pe.wait_ge(xn_ready, g * 8 + 8)
                after(pe, g_off_ready, g * 2 - 1)
                for t in range(TILES):
                    last = nc.tensor.transpose(front[2][:, t * P:(t + 1) * P], uh[:, t, :], eye)
                last.then_inc(ut_ps, 1)
                after(pe, g_off_ready, g * 2)
                for t in range(TILES):
                    last = nc.tensor.transpose(front[1][:, t * P:(t + 1) * P], xn[p][:, t, :], eye)
                last.then_inc(xnt_ps, 1)

            transpose_inputs(0, 0)

            def step(s, p, full=False):
                n, f, b, o = (True,) * 4 if full else (s + 1 < GROUPS, s < GROUPS, 1 <= s <= GROUPS, s >= 2)
                g, gb, go, pb = s, s - 1, s - 2, 1 - p
                if f:
                    pe.wait_ge(ut_ready, g + 1)
                    after(pe, z_done, g * 2 - 1)
                    project_xs(p, 0)
                    pe.wait_ge(xnt_ready, g + 1)
                    after(pe, z_done, g * 2)
                    project_xs(p, 1)
                if b:
                    pe.wait_ge(rows_ready, gb + 1)
                    spread(gb, pb, 0)
                    spread(gb, pb, 1)
                if f:
                    after(pe, rows_ready, g)
                    project_xs(p, 2)
                    pe.wait_ge(xs_taken, g * 4 + 1)
                    project_xs(p, 3)
                if b:
                    spread(gb, pb, 2)
                    after(pe, yz_first_ready, gb * 2)
                    after(pe, y_sum_ready, gb * 2)
                    for c in range(HALVES):
                        last = mm(y_ps[c][:, :], w_skip[:, c * P:(c + 1) * P], u_t[pb][:, :], start=True, stop=True,
                                  skip_group_check=True)
                    last.then_inc(skip_done, 1)
                if b:
                    pe.wait_ge(dtx_ready, gb + 1)
                    apply_mask(gb, pb, 0)
                if f:
                    pe.wait_ge(xs_taken, g * 4 + 2)
                    mm(front[1][:, :], w_in[:, W_BC:W_BC + P], u_t[p][:, :], start=True, stop=True).then_inc(bc_ps, 1)
                if b:
                    spread(gb, pb, 3)
                if o:
                    pe.wait_ge(yz_first_ready, go * 2 + 2)
                    pe.wait_ge(yz_second_ready, go + 1)
                    pe.wait_ge(rkv_ready, s if full else min(s, GROUPS))
                    mm(misc[:, :], share_b, row_parts[:, XD:XD + D].unsqueeze(1).to_broadcast([BIAS_ROWS, TILES, D]),
                       start=True, stop=True, skip_group_check=True)
                    for t in range(TILES):
                        for c in range(HALVES):
                            at = W_O + c * D
                            last = mm(misc[:, t * P:(t + 1) * P], yz[:, c, t * P:(t + 1) * P], wraw[:, at:at + D],
                                      start=False, stop=True, skip_group_check=True)
                    last.then_inc(out_ps, 1)
                if f:
                    pe.wait_ge(xs_taken, g * 4 + 3)
                    pe.wait_ge(xk_ready, g + 1)
                    mm(front[0][:, :], wraw[:, W_K:W_K + P], xk_t[:, :, :], start=True, stop=True).then_inc(k_ps, 1)
                if b:
                    apply_mask(gb, pb, 1)
                    spread(gb, pb, 4)
                if f:
                    pe.wait_ge(xs_taken, g * 4 + 4)
                    pe.wait_ge(bc_ready, g * 2 + 2)
                    for q in range(SEQS):
                        a = q * SEQ
                        mm(front[2 - q][:, 0:SEQ], b_t[:, a:a + P], c_t[:, a:a + SEQ], start=True, stop=True)
                        mm(front[2 - q][:, SEQ:SEQ + P], b_t[:, a + P:a + SEQ], c_t[:, a + P:a + SEQ],
                           start=True, stop=True).then_inc(g_ps, 1)
                if b:
                    apply_mask(gb, pb, 2)
                    if o:
                        pe.wait_ge(gated_out_ready, go + 1)
                    for c in range(HALVES):
                        last = mm(misc[:, c * 2 * P:(c + 1) * 2 * P], sel_half[:, c, :], decay_rows[pb][0:24, TOK:TOK + SEQS * P],
                                  start=True, stop=True)
                    last.then_inc(p_ps, 1)
                if f:
                    pe.wait_ge(xr_ready, g + 1)
                    pe.wait_ge(k_relu_ready, g + 1)
                    for t in range(TILES):
                        last = mm(front[0][:, t * P:(t + 1) * P], xr_t[:, t // 2, (t % 2) * P:(t % 2 + 1) * P],
                                  wraw[:, W_R:W_R + P], start=True, stop=True)
                    last.then_inc(r_ps, 1)
                if b:
                    spread(gb, pb, 5)
                    apply_mask(gb, pb, 3)
                    pe.wait_ge(p_ready, gb + 1)
                    pe.wait_ge(dtx_r_ready, gb + 1)
                    pe.wait_ge(g_off_ready, gb * 2 + 2)
                    for c in range(HALVES):
                        for q in range(SEQS):
                            last = mm(misc[:, (c * SEQS + q) * P:(c * SEQS + q + 1) * P], dtx_r[pb][:, q, c * P:(c + 1) * P],
                                      g_off[pb][:, q, :], start=True, stop=True)
                    last.then_inc(off_ps, 1)
                    apply_mask(gb, pb, 4)
                    spread(gb, pb, 6)
                if n:
                    transpose_inputs(g + 1, 1 - p)
                if f:
                    if b:
                        pe.wait_ge(off_ready, gb + 1)
                    pe.wait_ge(k_act_ready, g + 1)
                    for t in range(TILES):
                        last = mm(misc[:, t * P:(t + 1) * P], k_act[:, t * P:(t + 1) * P], w_v[:, :], start=True, stop=True)
                    last.then_inc(v_ps, 1)
                    pe.wait_ge(r_tanh_ready, g + 1)
                    pe.wait_ge(dt_parts_ready, g + 1)
                    for m, (mask, t0) in enumerate(((upto_b, 1), (after_b, 0))):
                        for part in range(3):
                            last = mm(front[0][:, m * 16:m * 16 + 16], mask, dt_a_parts[:, part, t0:TILES:2, :],
                                      start=(part == 0), stop=(part == 2))
                    last.then_inc(sums_ps, 1)
                    if n:
                        pe.wait_ge(ut_ready, g + 2)
                    else:
                        pe.wait_ge(g_off_ready, g * 2 + 1)
                    mm(front[2][:, :], w_in[:, W_Z:W_Z + P], u_t[p][:, :], start=True, stop=True).then_inc(z_ps, 1)
                if b:
                    spread(gb, pb, 7)
                    apply_mask(gb, pb, 5)
                if f:
                    if n:
                        pe.wait_ge(xnt_ready, g + 2)
                    else:
                        pe.wait_ge(g_off_ready, g * 2 + 2)
                    mm(front[1][:, :], w_in[:, W_Z + P:W_Z + 2 * P], u_t[p][:, :], start=True, stop=True).then_inc(z_ps, 1)
                if b:
                    apply_mask(gb, pb, 6)
                if f:
                    pe.wait_ge(parts_ready, g + 1)
                    pe.wait_ge(decays_ready, g * 2 + 2)
                    for t in range(TILES + SEQS):
                        last = nc.tensor.transpose(rows_ps[:, t * P:(t + 1) * P], decay_parts[:, t, :], eye_b)
                    last.then_inc(rows_done, 1)
                if b:
                    apply_mask(gb, pb, 7)

            steps(pe, step)

        @block.scalar
        def _(act):
            fn = nc.scalar.activation
            act.wait_ge(consts_in, 80)
            fn(neg_a[:, :], rowc[:, R_ALOG:R_ALOG + HEADS], ACT.Exp).then_inc(setup_act, 1)

            act.wait_ge(setup_dve, 2)

            def normalise(g, p):
                act.wait_ge(xc_ready, g * 2 + 2)
                after(act, xnt_ps, g)
                after(act, ut_ps, g)
                after(act, gated_xn_ready, g - 1)
                for kind, dst in ((1, uh), (0, xn[p])):
                    for t in range(TILES):
                        fn(dst[:, t, :], xc[:, t, :], ACT.Copy, scale=rstd[:, kind, t:t + 1]).then_inc(xn_ready, 1)

            def inputs_transposed(g, p):
                act.wait_ge(ut_ps, g + 1)
                after(act, skip_done, g - 1)
                fn(u_t[p][:, :], front[2][:, :], ACT.Copy).then_inc(ut_ready, 1)
                act.wait_ge(xnt_ps, g + 1)
                after(act, xk_ready, g)
                after(act, xr_ready, g)
                fn(xn_t[:, :, 1:SEQ + 1], front[1][:, :].rearrange("p (q t) -> p q t", q=SEQS), ACT.Copy).then_inc(xnt_ready, 1)

            normalise(0, 0)
            inputs_transposed(0, 0)

            def step(s, p, full=False):
                n, f, b = (True,) * 3 if full else (s + 1 < GROUPS, s < GROUPS, 1 <= s <= GROUPS)
                g, gb = s, s - 1
                if f:
                    after(act, dtx_ready, g)
                    for t in range(TILES):
                        act.wait_ge(xs_ps, g * 4 + t + 1)
                        fn(xs_dt[:, t, :], front[(2 - t) % 3][:, 0:XD], ACT.Copy).then_inc(xs_taken, 1)
                    act.wait_ge(xs_taken, g * 4 + 4)
                    after(act, dt_ready, g)
                    fn(dt_abs[:, :, :], xs_dt[:, :, INNER:XD], ACT.Abs).then_inc(dt_abs_ready, 1)
                    act.wait_ge(dt_abs_ready, g + 1)
                    fn(dt_exp[:, :, :], dt_abs[:, :, :], ACT.Exp, scale=-1.0).then_inc(dt_exp_ready, 1)
                    act.wait_ge(bc_ps, g + 1)
                    after(act, g_ps, g * 2)
                    fn(b_t[:, :], front[1][0:STATE, :], ACT.Identity, bias=bias_col[0:STATE, 2:3]).then_inc(bc_ready, 1)
                    fn(c_t[:, :], front[1][STATE:P, :], ACT.Identity, bias=bias_col[STATE:P, 2:3]).then_inc(bc_ready, 1)
                    act.wait_ge(k_ps, g + 1)
                    fn(k_relu[:, :], front[0][:, :], ACT.Relu).then_inc(k_relu_ready, 1)
                    after(act, mask_dve, (g - 1) * len(DVE_HEADS))
                    after(act, mask_pool, (g - 1) * len(POOL_HEADS))
                    after(act, off_ps, g - 1)
                    for q in range(SEQS):
                        act.wait_ge(g_ps, g * 2 + q + 1)
                        products = front[2 - q][:, :].rearrange("p (t i) -> p t i", i=SEQ)
                        fn(g_diag[p][:, 2 * q:2 * q + 2, :], products[:, :, 0:P], ACT.Copy).then_inc(g_diag_ready, 1)
                        fn(g_off[p][:, q, :], products[:, 0, P:SEQ], ACT.Copy).then_inc(g_off_ready, 1)
                if b:
                    act.wait_ge(p_ps, gb + 1)
                    after(act, off_ready, gb)
                    fn(p_bc[:, :, :, :], misc[:, :].rearrange("p (c q t) -> p c q t", c=HALVES, q=SEQS), ACT.Copy).then_inc(p_ready, 1)
                if n:
                    normalise(g + 1, 1 - p)
                if f:
                    act.wait_ge(k_relu_ready, g + 1)
                    after(act, v_ps, g)
                    fn(k_act[:, :], k_relu[:, :], ACT.Square).then_inc(k_act_ready, 1)
                    act.wait_ge(r_ps, g + 1)
                    after(act, rkv_ready, g)
                    fn(r_tanh[:, :], front[0][:, :], ACT.Tanh, scale=0.5).then_inc(r_tanh_ready, 1)
                if n:
                    inputs_transposed(g + 1, 1 - p)
                if f:
                    act.wait_ge(dt_a_ready, g + 1)
                    after(act, parts_ready, g)
                    after(act, dtx_r_ready, g)
                    fn(decays[:, 0:TILES, :], dt_a[:, :, :], ACT.Exp, bias=colc[:, C_RESET:C_RESET + 1]).then_inc(decays_ready, 1)
                    act.wait_ge(sums_ps, g + 1)
                    fn(decays[:, TILES:TILES + 2 * SEQS, :], front[0][:, 0:32].rearrange("p (t h) -> p t h", h=HEADS),
                       ACT.Exp).then_inc(decays_ready, 1)
                    after(act, yz_second_ready, g - 1)
                    fn(table_warm[:, 1:2], neg_a[:, 0:1], ACT.Silu)
                    act.wait_ge(z_ps, g * 2 + 1)
                    fn(z_silu[p][:, 0, :], front[2][:, :], ACT.Silu, bias=bias_col[:, 0:1]).then_inc(z_done, 1)
                    act.wait_ge(z_ps, g * 2 + 2)
                    fn(z_silu[p][:, 1, :], front[1][:, :], ACT.Silu, bias=bias_col[:, 1:2]).then_inc(z_done, 1)
                    act.wait_ge(rows_done, g + 1)
                    after(act, bcast_ps, (g - 1) * 8)
                    after(act, p_ps, g - 1)
                    fn(decay_rows[p][:, :], rows_ps, ACT.Copy).then_inc(rows_ready, 1)
                    act.wait_ge(rkv_ready, g + 1)
                    after(act, gated_out_ready, g - 1)
                    fn(gate[p][:, :], rkv[:, :], ACT.Silu).then_inc(gate_ready, 1)
                    if n:
                        fn(table_warm[:, 0:1], neg_a[:, 0:1], ACT.Exp)

            steps(act, step)

        @block.gpsimd
        def _(pool):
            tt = nc.gpsimd.tensor_tensor
            nc.gpsimd.memset(xn_t[:, :, 0:1], 0.0)
            nc.gpsimd.memset(zeros[:, :, :], 0.0)
            nc.gpsimd.memset(decay_parts[:, :, 24:32], 0.0)
            nc.gpsimd.memset(minus_half[:, :, :], -0.5).then_inc(setup_pool, 1)
            pool.wait_ge(setup_pool, 1)
            pool.wait_ge(consts_in, 80)

            def per_tile(column):
                return column.unsqueeze(2).to_broadcast([P, TILES, D])

            def normalise(g):
                pool.wait_ge(var_ready, g * 2 + 2)
                at = bass.ds(g * TILES, TILES)
                after(pool, xn_ready, g * 8)
                tt(rstd[:, :, :], variances[:, :, :], minus_half[:, :, :], ALU.pow).then_inc(xc_ready, 1)
                tt(xc[:, :, :], x_all[:, at, :], per_tile(mean[:, :]), ALU.subtract).then_inc(xc_ready, 1)

            def mask_head(b, p, h):
                pool.wait_ge(scan_done, b * 8 + h + 1)
                pool.wait_ge(g_diag_ready, b * 2 + 2)
                tt(masks[:, h % SLOTS, :], masks[:, h % SLOTS, :], g_diag[p][:, :, :].rearrange("p t i -> p (t i)"),
                   ALU.mult).then_inc(mask_pool, 1)

            def difference(g):
                pool.wait_ge(xnt_ready, g + 1)
                after(pool, xk_ready, g)
                after(pool, xr_ready, g)
                tt(diff[:, :, :], xn_t[:, :, 1:SEQ + 1], xn_t[:, :, 0:SEQ], ALU.subtract).then_inc(diff_ready, 1)

            pool.wait_ge(setup_dve, 2)
            normalise(0)
            difference(0)

            def step(s, p, full=False):
                n, f, b, o = (True,) * 4 if full else (s + 1 < GROUPS, s < GROUPS, 1 <= s <= GROUPS, s >= 2)
                g, gb, go, pb = s, s - 1, s - 2, 1 - p
                if o:
                    pool.wait_ge(y_sum_ready, go * 2 + 2)
                    pool.wait_ge(z_done, go * 2 + 2)
                    after(pool, out_ps, go)
                    for c in range(HALVES):
                        at = yz[:, c, :].rearrange("p (q a i) -> p q a i", q=SEQS, a=2)[:, :, 1, :]
                        z = z_silu[p][:, c, :].rearrange("p (q a i) -> p q a i", q=SEQS, a=2)[:, :, 1, :]
                        last = tt(at, y_sum[:, c, :, :], z, ALU.mult)
                    last.then_inc(yz_second_ready, 1)
                if b:
                    pool.wait_ge(gate_ready, gb + 1)
                    tt(gated_xn[:, :, :], xn[pb][:, :, :], gate[pb][:, :].rearrange("p (t d) -> p t d", d=D),
                       ALU.mult).then_inc(gated_xn_ready, 1)
                    mask_head(gb, pb, 1)
                if n:
                    normalise(g + 1)
                if b:
                    mask_head(gb, pb, 3)
                    pool.wait_ge(gated_xn_ready, gb + 1)
                    x_b = x_all[:, bass.ds(gb * TILES, TILES), :]
                    tt(x_b, gated_xn[:, :, :], x_b, ALU.add).then_inc(residual_ready, 1)
                if f:
                    pool.wait_ge(dt_ready, g + 1)
                    after(pool, y_done, (g - 1) * 8)
                    for t in range(TILES):
                        last = tt(dtx[p][:, t, :].rearrange("p (h e) -> p h e", h=HEADS),
                                  xs_dt[:, t, 0:INNER].rearrange("p (h e) -> p h e", h=HEADS),
                                  dt[:, t, :].unsqueeze(2).to_broadcast([P, HEADS, HEAD_DIM]), ALU.mult)
                    last.then_inc(dtx_ready, 1)
                if b:
                    mask_head(gb, pb, 5)
                if f:
                    pool.wait_ge(decays_ready, g * 2 + 2)
                    after(pool, rows_done, g)
                    wide, part = decays[:, 0:TILES + SEQS, :], decay_parts
                    tt(part[:, :, 0:8], wide, zeros[:, :, :], ALU.add).then_inc(split_chain, 1)
                    pool.wait_ge(split_chain, g * 3 + 1)
                    tt(decays_rest[:, :, :], wide, part[:, :, 0:8], ALU.subtract).then_inc(split_chain, 1)
                    pool.wait_ge(split_chain, g * 3 + 2)
                    tt(part[:, :, 8:16], decays_rest[:, :, :], zeros[:, :, :], ALU.add).then_inc(split_chain, 1)
                    pool.wait_ge(split_chain, g * 3 + 3)
                    tt(part[:, :, 16:24], decays_rest[:, :, :], part[:, :, 8:16], ALU.subtract).then_inc(parts_ready, 1)
                if n:
                    difference(g + 1)
                if f:
                    pool.wait_ge(dtx_ready, g + 1)
                    after(pool, off_ps, g - 1)
                    for q in range(SEQS):
                        last = tt(dtx_r[p][:, q, :].rearrange("p (h e) -> p h e", h=HEADS),
                                  dtx[p][:, 2 * q, :].rearrange("p (h e) -> p h e", h=HEADS),
                                  decays[:, TILES + SEQS + q, :].unsqueeze(2).to_broadcast([P, HEADS, HEAD_DIM]), ALU.mult)
                    last.then_inc(dtx_r_ready, 1)

            steps(pool, step)

        @block.vector
        def _(dve):
            v = nc.vector
            SETUP = 28
            dve.wait_ge(consts_in, 80)
            v.tensor_copy(xc[:, 0, :], colc[:, C_BETA:C_BETA + 1].to_broadcast([P, P])).then_inc(setup_dve, 1)
            v.tensor_scalar(w_in[:, :], wraw[:, 0:W_K], colc[:, C_GAMMA:C_GAMMA + 1], None, ALU.mult).then_inc(dt_chain, 1)
            v.tensor_scalar(w_v[:, :], wraw[:, W_V:W_V + D], 0.5, None, ALU.mult)
            dve.wait_ge(dt_chain, 1)
            v.tensor_tensor(w_skip[:, :].rearrange("p (h e) -> p h e", h=HEADS),
                            w_in[:, W_XD:W_XD + INNER].rearrange("p (h e) -> p h e", h=HEADS),
                            rowc[:, R_DROW:R_DROW + HEADS].unsqueeze(2).to_broadcast([P, HEADS, HEAD_DIM]), ALU.mult)
            dve.wait_ge(setup_pe, 1)
            v.tensor_tensor(bias_col[:, :], misc[:, 0:5], colc[:, C_BZ:C_BZ + 5], ALU.add).then_inc(dt_chain, 1)
            v.tensor_tensor(bias_xd[:, :], misc[:, P:P + XD], rowc[:, R_BXD:R_BXD + XD], ALU.add).then_inc(dt_chain, 1)
            dve.wait_ge(dt_chain, 3)
            v.tensor_tensor(bias_col[:, 3:5], bias_col[:, 3:5], colc[:, C_DSK:C_DSK + 2], ALU.mult)
            v.tensor_tensor(bias_xd[:, INNER:XD], bias_xd[:, INNER:XD], rowc[:, R_DTB:R_DTB + HEADS], ALU.add).then_inc(dt_chain, 1)
            dve.wait_ge(dt_chain, 4)
            done = 4
            for n in range(3):
                for rows_, at, width in ((bias_xd[:, :], 0, XD), (rowc[:, R_BOUT:R_BOUT + D], XD, D)):
                    lanes = slice(32 * n, 32 * n + 32)
                    rest, part = row_rest[lanes, at:at + width], row_parts[lanes, at:at + width]
                    v.tensor_copy(rest, rows_[lanes, :]).then_inc(dt_chain, 1)
                    done += 1
                    for _ in range(n):
                        dve.wait_ge(dt_chain, done)
                        v.tensor_copy(part, rest).then_inc(dt_chain, 1)
                        dve.wait_ge(dt_chain, done + 1)
                        v.tensor_tensor(rest, rest, part, ALU.subtract).then_inc(dt_chain, 1)
                        done += 2
                    dve.wait_ge(dt_chain, done)
                    v.tensor_copy(part, rest).then_inc(dt_chain, 1)
                    done += 1
            assert done == SETUP
            dve.wait_ge(dt_chain, done)
            dve.wait_ge(setup_act, 1)
            v.tensor_scalar(neg_a[:, :], neg_a[:, :], -1.0, None, ALU.mult).then_inc(setup_dve, 1)
            dve.wait_ge(setup_dve, 2)


            def norm_stats(g, i, t):
                if t == 0:
                    dve.wait_ge(x_in[i], g * 8 + (16 - 8 * i))
                    after(dve, norm_chain, g * 9)
                v.bn_stats(stats[:, t, :], x_all[:, bass.ds(g * TILES + t, 1), :].rearrange("p o d -> p (o d)")).then_inc(norm_chain, 1)

            m_even, q_even, m_odd, q_odd = (stats[:, :, k] for k in (1, 2, 4, 5))

            def norm_gaps(g):
                dve.wait_ge(norm_chain, g * 9 + 4)
                v.tensor_tensor(m_gap[:, :], m_even, m_odd, ALU.subtract).then_inc(norm_chain, 1)
                v.tensor_tensor(q_sum[:, :], q_even, q_odd, ALU.add).then_inc(norm_chain, 1)

            def norm_mean(g):
                dve.wait_ge(norm_chain, g * 9 + 6)
                after(dve, xc_ready, g * 2)
                v.scalar_tensor_tensor(out=mean[:, :], in0=m_gap[:, :], scalar=-0.5, in1=m_even,
                                       op0=ALU.mult, op1=ALU.add).then_inc(norm_chain, 1)
                v.tensor_tensor(m_gap2[:, :], m_gap[:, :], m_gap[:, :], ALU.mult).then_inc(norm_chain, 1)

            def norm_deviations(g):
                dve.wait_ge(norm_chain, g * 9 + 8)
                v.scalar_tensor_tensor(out=q_all[:, :], in0=m_gap2[:, :], scalar=D / 4.0, in1=q_sum[:, :],
                                       op0=ALU.mult, op1=ALU.add).then_inc(norm_chain, 1)

            def norm_variances(g):
                dve.wait_ge(norm_chain, g * 9 + 9)
                v.tensor_scalar(variances[:, 0, :], q_all[:, :], 1.0 / D, EPS, ALU.mult, ALU.add).then_inc(var_ready, 1)
                v.tensor_scalar(variances[:, 1, :], q_all[:, :], (1.0 + EPS) / D, EPS * EPS, ALU.mult, ALU.add).then_inc(var_ready, 1)

            def scan(b, h):
                dve.wait_ge(bcast_ps, b * 8 + h + 1)
                after(dve, y_done, b * 8 + (h + 1 - SLOTS))
                v.tensor_tensor_scan(masks[:, h % SLOTS, :], bcast[h % 2][:, :], eye4, 0.0, ALU.mult, ALU.add).then_inc(scan_done, 1)

            def mask_head(b, p, h):
                dve.wait_ge(scan_done, b * 8 + h + 1)
                dve.wait_ge(g_diag_ready, b * 2 + 2)
                v.tensor_tensor(masks[:, h % SLOTS, :], masks[:, h % SLOTS, :],
                                g_diag[p][:, :, :].rearrange("p t i -> p (t i)"), ALU.mult).then_inc(mask_dve, 1)

            def log1p(g, k):
                done = LOG1P_DEG - k
                q, e = poly[:, k % 2, :, :], dt_exp[:, :, :]
                if k == LOG1P_DEG:
                    dve.wait_ge(dt_exp_ready, g + 1)
                    v.tensor_scalar(q, e, coef[k], None, ALU.mult).then_inc(dt_chain, 1)
                else:
                    dve.wait_ge(dt_chain, g * 12 + (SETUP + done))
                    v.scalar_tensor_tensor(out=q, in0=poly[:, (k + 1) % 2, :, :], scalar=coef[k], in1=e,
                                           op0=ALU.add, op1=ALU.mult).then_inc(dt_chain, 1)

            def dt_value(g):
                dve.wait_ge(dt_chain, g * 12 + (SETUP + LOG1P_DEG + 1))
                v.scalar_tensor_tensor(out=dt[:, :, :], in0=xs_dt[:, :, INNER:XD], scalar=0.0, in1=poly[:, 0, :, :],
                                       op0=ALU.max, op1=ALU.add).then_inc(dt_ready, 1)

            def dt_decay(g):
                dve.wait_ge(dt_ready, g + 1)
                after(dve, decays_ready, g * 2)
                v.tensor_tensor(dt_a[:, :, :], dt[:, :, :], neg_a[:, :].unsqueeze(1).to_broadcast([P, TILES, HEADS]),
                                ALU.mult).then_inc(dt_a_ready, 1)

            def dt_part(g, n):
                part, rest = dt_a_parts, dt_a_rest[:, :, :]
                if n == 0:
                    dve.wait_ge(dt_a_ready, g + 1)
                    after(dve, sums_ps, g)
                    v.tensor_copy(part[:, 0, :, :], dt_a[:, :, :]).then_inc(dt_chain, 1)
                else:
                    dve.wait_ge(dt_chain, g * 12 + (SETUP + LOG1P_DEG + 1 + n))
                if n == 1:
                    v.tensor_tensor(rest, dt_a[:, :, :], part[:, 0, :, :], ALU.subtract).then_inc(dt_chain, 1)
                if n == 2:
                    v.tensor_copy(part[:, 1, :, :], rest).then_inc(dt_chain, 1)
                if n == 3:
                    v.tensor_tensor(part[:, 2, :, :], rest, part[:, 1, :, :], ALU.subtract).then_inc(dt_parts_ready, 1)

            def mix(g, mu, dst, done, used):
                dve.wait_ge(diff_ready, g + 1)
                after(dve, used, g)
                v.scalar_tensor_tensor(out=dst[:, :, :], in0=diff[:, :, :], scalar=colc[:, mu:mu + 1], in1=xn_t[:, :, 0:SEQ],
                                       op0=ALU.mult, op1=ALU.add).then_inc(done, 1)

            def read_y(b, p):
                dve.wait_ge(y_done, b * 8 + 8)
                dve.wait_ge(off_ready, b + 1)
                dve.wait_ge(z_done, b * 2 + 2)
                after(dve, out_ps, b)
                after(dve, yz_second_ready, b)
                for c in range(HALVES):
                    y = y_ps[c][:, :].rearrange("p (q a i) -> p q a i", q=SEQS, a=2)
                    z = z_silu[p][:, c, :].rearrange("p (q a i) -> p q a i", q=SEQS, a=2)
                    dst = yz[:, c, :].rearrange("p (q a i) -> p q a i", q=SEQS, a=2)
                    v.scalar_tensor_tensor(out=y_sum[:, c, :, :], in0=y[:, :, 1, :], scalar=bias_col[:, 3 + c:4 + c],
                                           in1=y_off[:, c, :, :], op0=ALU.add, op1=ALU.add).then_inc(y_sum_ready, 1)
                    v.scalar_tensor_tensor(out=dst[:, :, 0, :], in0=y[:, :, 0, :], scalar=bias_col[:, 3 + c:4 + c],
                                           in1=z[:, :, 0, :], op0=ALU.add, op1=ALU.mult).then_inc(yz_first_ready, 1)

            def gate_output(o, p):
                dve.wait_ge(out_ps, o + 1)
                dve.wait_ge(gate_ready, o + 1)
                v.tensor_tensor(gated_out[:, :], misc[:, :], gate[p][:, :], ALU.mult).then_inc(gated_out_ready, 1)

            def add_residual(o):
                dve.wait_ge(gated_out_ready, o + 1)
                dve.wait_ge(residual_ready, o + 1)
                x_o = x_all[:, bass.ds(o * TILES, TILES), :]
                v.tensor_tensor(x_o, gated_out[:, :].rearrange("p (t d) -> p t d", d=D), x_o, ALU.add).then_inc(final_ready, 1)

            def scale_off(b):
                dve.wait_ge(off_ps, b + 1)
                dve.wait_ge(p_ready, b + 1)
                v.tensor_tensor(y_off[:, :, :, :].rearrange("p c q i -> p (c q i)"), misc[:, :],
                                p_bc[:, :, :, :].rearrange("p c q i -> p (c q i)"), ALU.mult).then_inc(off_ready, 1)

            def multiply_rkv(g):
                dve.wait_ge(v_ps, g + 1)
                dve.wait_ge(r_tanh_ready, g + 1)
                after(dve, gate_ready, g)
                v.scalar_tensor_tensor(out=rkv[:, :], in0=r_tanh[:, :], scalar=1.0, in1=misc[:, :],
                                       op0=ALU.add, op1=ALU.mult).then_inc(rkv_ready, 1)

            for t in range(TILES):
                norm_stats(0, 0, t)
            norm_gaps(0)
            norm_mean(0)
            norm_deviations(0)
            norm_variances(0)

            def step(s, p, full=False):
                n, f, b, o = (True,) * 4 if full else (s + 1 < GROUPS, s < GROUPS, 1 <= s <= GROUPS, s >= 2)
                g, gb, go, pb = s, s - 1, s - 2, 1 - p
                if b:
                    scan(gb, 0)
                if n:
                    norm_stats(g + 1, 1 - p, 0)
                    norm_stats(g + 1, 1 - p, 1)
                if b:
                    scan(gb, 1)
                    mask_head(gb, pb, 0)
                if n:
                    norm_stats(g + 1, 1 - p, 2)
                    norm_stats(g + 1, 1 - p, 3)
                if f:
                    mix(g, C_MUK, xk_t, xk_ready, k_ps)
                if n:
                    norm_gaps(g + 1)
                if b:
                    scan(gb, 2)
                if n:
                    norm_mean(g + 1)
                if f:
                    log1p(g, 8)
                if b:
                    mask_head(gb, pb, 2)
                if n:
                    norm_deviations(g + 1)
                if f:
                    log1p(g, 7)
                if b:
                    scan(gb, 3)
                if n:
                    norm_variances(g + 1)
                if f:
                    log1p(g, 6)
                    log1p(g, 5)
                    mix(g, C_MUR, xr_t, xr_ready, r_ps)
                    log1p(g, 4)
                    log1p(g, 3)
                if o:
                    gate_output(go, p)
                if f:
                    log1p(g, 2)
                    log1p(g, 1)
                if b:
                    scan(gb, 4)
                if f:
                    log1p(g, 0)
                    dt_value(g)
                if b:
                    mask_head(gb, pb, 4)
                if f:
                    dt_decay(g)
                    dt_part(g, 0)
                if o:
                    add_residual(go)
                if f:
                    dt_part(g, 1)
                if b:
                    scan(gb, 5)
                if f:
                    dt_part(g, 2)
                    dt_part(g, 3)
                if b:
                    scale_off(gb)
                    scan(gb, 6)
                    mask_head(gb, pb, 6)
                if f:
                    multiply_rkv(g)
                if b:
                    scan(gb, 7)
                    mask_head(gb, pb, 7)
                    read_y(gb, pb)

            steps(dve, step)


def constants():
    k, m = np.indices((P, P))
    f32 = np.tile(np.eye(P), (1, TILES)).astype(np.float32)
    row = np.arange(P)[:, None]
    real = row < 24
    head_of = np.where(real, row % HEADS, -1)
    sel_head = np.concatenate([np.repeat(head_of == h, P, axis=1) for h in range(HEADS)], axis=1)
    sel_half = head_of == (np.arange(INNER) // HEAD_DIM)[None, :]
    b16 = np.concatenate([k == m, k <= m, k > m, sel_head, sel_half, np.full((P, P), 1 / 32)], axis=1)
    return f32, b16.astype(mybir.dt.np(BF16))


def kernel(L0_attn_input_tensor, L0_attn_ln_gamma, L0_attn_ln_beta, L0_attn_W_in, L0_attn_b_in, L0_attn_A_log, L0_attn_D_skip,
           L0_attn_dt_bias, L0_attn_W_out, L0_attn_b_out, L0_ffn_W_r, L0_ffn_W_k, L0_ffn_W_v, L0_ffn_mu_r, L0_ffn_mu_k):
    import concourse.bacc as bacc
    from concourse.bass_utils import run_bass_kernel_spmd

    x = np.ascontiguousarray(np.asarray(L0_attn_input_tensor)).reshape(BATCH * SEQ, D)
    w_in, b_in = np.asarray(L0_attn_W_in), np.asarray(L0_attn_b_in)
    z, xs, bc_, dt = slice(0, INNER), slice(INNER, 2 * INNER), slice(2 * INNER, 2 * INNER + 2 * STATE), slice(2 * INNER + 2 * STATE, None)
    w_out = np.asarray(L0_attn_W_out)
    weights = np.concatenate([w_in[:, z], w_in[:, xs], w_in[:, dt], w_in[:, bc_], np.asarray(L0_ffn_W_k).T, np.asarray(L0_ffn_W_r).T,
                              np.asarray(L0_ffn_W_v).T] + [w_out[c * P:(c + 1) * P] for c in range(HALVES)], axis=1)
    reset = np.zeros(P, np.float32)
    reset[0] = -30000.0
    skip = np.repeat(np.asarray(L0_attn_D_skip), HEAD_DIM)
    cols = np.stack([np.asarray(L0_attn_ln_gamma), np.asarray(L0_attn_ln_beta), np.asarray(L0_ffn_mu_r), np.asarray(L0_ffn_mu_k),
                     b_in[0:P], b_in[P:2 * P], b_in[bc_], b_in[xs][:P], b_in[xs][P:], skip[:P], skip[P:], reset], axis=1)
    row = np.concatenate([b_in[xs], b_in[dt], np.asarray(L0_attn_dt_bias), np.asarray(L0_attn_A_log), np.asarray(L0_attn_b_out),
                          np.asarray(L0_attn_D_skip)])
    rows = np.tile(row[None, :], (P, 1))
    f32_consts, bf16_consts = constants()
    arrays = {"x": x, "weights": weights, "cols": cols, "rows": rows, "f32_consts": f32_consts, "bf16_consts": bf16_consts}
    arrays = {k: np.ascontiguousarray(a) for k, a in arrays.items()}

    nc = bacc.Bacc("TRN2", target_bir_lowering=False, num_devices=1)
    args = [nc.dram_tensor(n, list(a.shape), mybir.dt.from_np(a.dtype), kind="ExternalInput").ap() for n, a in arrays.items()]
    out = nc.dram_tensor("out", [BATCH * SEQ, D], F32, kind="ExternalOutput").ap()
    build(nc, *args, out)
    result = run_bass_kernel_spmd(nc, [arrays], core_ids=[0])
    return result.results[0]["out"].reshape(BATCH, SEQ, D)
```

```python
from contextlib import ExitStack

import numpy as np

import concourse.bass as bass
from concourse import mybir

P = 128
F32 = mybir.dt.float32
BF16 = mybir.dt.bfloat16
ALU = mybir.AluOpType
ACT = mybir.ActivationFunctionType

BATCH, SEQ, D = 32, 256, 128
HEADS, HEAD_DIM, STATE = 8, 32, 64
INNER = HEADS * HEAD_DIM
TILES = 4
SEQS = TILES * P // SEQ
GROUPS = BATCH * SEQ // (TILES * P)
TOK = TILES * P
XD = INNER + HEADS
EPS = 1e-5
LOG1P_DEG = 8
SLOTS = 8
POOL_HEADS = (1, 3, 5)
DVE_HEADS = tuple(h for h in range(HEADS) if h not in POOL_HEADS)
HALVES = INNER // P

C_GAMMA, C_BETA, C_MUR, C_MUK, C_BZ, C_BBC, C_BXS, C_DSK, C_RESET = 0, 1, 2, 3, 4, 6, 7, 9, 11
NCOL = 12
R_BDT, R_DTB, R_ALOG, R_BOUT = 0, HEADS, 2 * HEADS, 3 * HEADS
NROW = 3 * HEADS + D
BIAS_ROWS = 96
W_Z, W_XD, W_BC, W_K, W_R, W_V, W_O = 0, INNER, INNER + XD, INNER + XD + P, INNER + XD + 2 * P, INNER + XD + 3 * P, INNER + XD + 4 * P
NW = W_O + HALVES * D


def log1p_coefficients():
    n = LOG1P_DEG + 1
    x = 0.5 + 0.5 * np.cos((np.arange(n) + 0.5) * np.pi / n)
    return [float(c) for c in np.polynomial.Polynomial.fit(x, np.log1p(x) / x, LOG1P_DEG, domain=[0, 1], window=[0, 1]).coef]


def build(nc, x, weights, cols, rows, identity, bf16_consts, selectors, out):
    coef = log1p_coefficients()
    x_tiles = x.rearrange("(n p) d -> p n d", p=P)
    out_tiles = out.rearrange("(n p) d -> p n d", p=P)

    with ExitStack() as ctx:
        def sb(name, shape, dt=F32):
            return ctx.enter_context(nc.sbuf_tensor(name, shape, dt))

        def sem(name):
            return ctx.enter_context(nc.semaphore(name))

        def pair(name, shape, dt=F32):
            return [sb(f"{name}{i}", shape, dt) for i in range(2)]

        wraw = sb("wraw", [P, NW])
        colc = sb("colc", [P, NCOL])
        rowc = sb("rowc", [P, NROW])
        eyes = sb("eyes", [P, TOK])
        eye4 = eyes[:, :]
        eye = eyes[:, 0:P]
        triangles = sb("triangles", [P, 3 * P], BF16)
        sel = sb("sel", [24, (HEADS + HALVES) * P], BF16)
        share_b = sb("share_b", [BIAS_ROWS, P], BF16)
        eye_b = triangles[:, 0:P]
        upto_b = triangles[:, P:2 * P]
        after_b = triangles[:, 2 * P:3 * P]
        sel_head = sel[:, 0:HEADS * P].rearrange("k (h m) -> k h m", h=HEADS)
        sel_half = sel[:, HEADS * P:].rearrange("k (c m) -> k c m", c=HALVES)
        w_in = sb("w_in", [P, W_K])
        w_v = sb("w_v", [P, D])
        row_parts = sb("row_parts", [BIAS_ROWS, HEADS + D], BF16)
        row_rest = sb("row_rest", [BIAS_ROWS, HEADS + D])
        bias_col = sb("bias_col", [P, 6])
        table_warm = sb("table_warm", [P, 2])
        neg_a = sb("neg_a", [P, HEADS])

        x_all = sb("x_all", [P, GROUPS * TILES, D])
        stats = sb("stats", [P, TILES, 6])
        mean, m_gap, m_gap2, q_sum, q_all = (sb(n, [P, TILES]) for n in ("mean", "m_gap", "m_gap2", "q_sum", "q_all"))
        variances = sb("variances", [P, 2, TILES])
        minus_half = sb("minus_half", [P, 2, TILES])
        rstd = sb("rstd", [P, 2, TILES])
        xc = sb("xc", [P, TILES, D])
        xn = pair("xn", [P, TILES, D])
        uh = sb("uh", [P, TILES, D])
        xn_t = sb("xn_t", [P, SEQS, SEQ + 1])
        u_t = pair("u_t", [P, TOK])
        diff = sb("diff", [P, SEQS, SEQ])
        xr_t = sb("xr_t", [P, SEQS, SEQ])
        xk_t = sb("xk_t", [P, SEQS, SEQ])
        k_relu = sb("k_relu", [P, TOK])
        k_act = sb("k_act", [P, TOK])
        z_silu = pair("z_silu", [P, HALVES, TOK])
        b_t = sb("b_t", [STATE, TOK])
        c_t = sb("c_t", [STATE, TOK])
        xs_t = pair("xs_t", [P, HALVES, TOK])
        xs = sb("xs", [P, TILES, INNER])
        dt_raw = sb("dt_raw", [P, TILES, HEADS])
        dt_abs = sb("dt_abs", [P, TILES, HEADS])
        dt_exp = sb("dt_exp", [P, TILES, HEADS])
        poly = sb("poly", [P, 2, TILES, HEADS])
        dt = sb("dt", [P, TILES, HEADS])
        dt_a = sb("dt_a", [P, TILES, HEADS])
        dt_a_rest = sb("dt_a_rest", [P, TILES, HEADS])
        dt_a_parts = sb("dt_a_parts", [P, 3, TILES, HEADS], BF16)
        decays = sb("decays", [P, 4 + 2 * SEQS, HEADS])
        decays_rest = sb("decays_rest", [P, 4 + SEQS, HEADS])
        decay_parts = sb("decay_parts", [P, 4 + SEQS, 32], BF16)
        zeros = sb("zeros", [P, 4 + SEQS, HEADS])
        decay_rows = pair("decay_rows", [32, (4 + SEQS) * P], BF16)
        dtx = pair("dtx", [P, TILES, INNER])
        dtx_r = pair("dtx_r", [P, SEQS, INNER])
        g_diag = pair("g_diag", [P, TILES, P])
        g_off = pair("g_off", [P, SEQS, P])
        masks = sb("masks", [P, SLOTS, TOK])
        p_bc = sb("p_bc", [P, HALVES, SEQS, P])
        y_off = sb("y_off", [P, HALVES, SEQS, P])
        y_sum = sb("y_sum", [P, HALVES, SEQS, P])
        yz = sb("yz", [P, HALVES, TOK])
        r_tanh = sb("r_tanh", [P, TOK])
        rkv = sb("rkv", [P, TOK])
        gate = pair("gate", [P, TOK])
        gated_xn = sb("gated_xn", [P, TILES, D])
        gated_out = sb("gated_out", [P, TOK])

        front = [ctx.enter_context(nc.psum_tensor(f"front{i}", [P, 512], F32)) for i in range(3)]
        bcast = [ctx.enter_context(nc.psum_tensor(f"bcast{i}", [P, 512], F32)) for i in range(2)]
        y_ps = [ctx.enter_context(nc.psum_tensor(f"y_ps{i}", [P, 512], F32)) for i in range(2)]
        misc = ctx.enter_context(nc.psum_tensor("misc", [P, 512], F32))
        rows_ps = front[0][0:32, 0:(4 + SEQS) * P // 2].bitcast(BF16)

        x_in = [sem("x_in0"), sem("x_in1")]
        consts_in = sem("consts_in")
        stored = sem("stored")
        setup_pe, setup_dve, setup_act, setup_pool = sem("setup_pe"), sem("setup_dve"), sem("setup_act"), sem("setup_pool")
        norm_chain = sem("norm_chain")
        var_ready = sem("var_ready")
        xc_ready = sem("xc_ready")
        rstd_ready = sem("rstd_ready")
        uh_ready = sem("uh_ready")
        xn_ready = sem("xn_ready")
        xnt_ps, ut_ps = sem("xnt_ps"), sem("ut_ps")
        xnt_ready, ut_ready = sem("xnt_ready"), sem("ut_ready")
        diff_ready = sem("diff_ready")
        xr_ready, xk_ready = sem("xr_ready"), sem("xk_ready")
        xst_ps, xst_ready = sem("xst_ps"), sem("xst_ready")
        xs_ps, xs_ready = sem("xs_ps"), sem("xs_ready")
        dt_ps = sem("dt_ps")
        z_ps = sem("z_ps")
        z_done = sem("z_done")
        bc_ps = sem("bc_ps")
        bc_ready = sem("bc_ready")
        k_ps = sem("k_ps")
        k_relu_ready, k_act_ready = sem("k_relu_ready"), sem("k_act_ready")
        g_ps = sem("g_ps")
        g_diag_ready = sem("g_diag_ready")
        g_off_ready = sem("g_off_ready")
        dt_abs_ready, dt_exp_ready = sem("dt_abs_ready"), sem("dt_exp_ready")
        dt_chain = sem("dt_chain")
        dt_ready, dt_a_ready = sem("dt_ready"), sem("dt_a_ready")
        dt_parts_ready = sem("dt_parts_ready")
        sums_ps = sem("sums_ps")
        decays_ready = sem("decays_ready")
        split_chain = sem("split_chain")
        parts_ready = sem("parts_ready")
        rows_done = sem("rows_done")
        rows_ready = sem("rows_ready")
        dtx_ready, dtx_r_ready = sem("dtx_ready"), sem("dtx_r_ready")
        r_ps, v_ps = sem("r_ps"), sem("v_ps")
        r_tanh_ready, rkv_ready, gate_ready = sem("r_tanh_ready"), sem("rkv_ready"), sem("gate_ready")
        skip_done = sem("skip_done")
        bcast_ps = sem("bcast_ps")
        scan_done = sem("scan_done")
        mask_dve = sem("mask_dve")
        mask_pool = sem("mask_pool")
        y_done = sem("y_done")
        p_ps, p_ready = sem("p_ps"), sem("p_ready")
        off_ps, off_ready = sem("off_ps"), sem("off_ready")
        y_sum_ready = sem("y_sum_ready")
        yz_first_ready = sem("yz_first_ready")
        out_ps = sem("out_ps")
        yz_second_ready = sem("yz_second_ready")
        gated_xn_ready, residual_ready = sem("gated_xn_ready"), sem("residual_ready")
        gated_out_ready, final_ready = sem("gated_out_ready"), sem("final_ready")

        def after(eng, semaphore, value):
            if not isinstance(value, int) or value > 0:
                eng.wait_ge(semaphore, value)

        def steps(eng, body):
            for s in range(3):
                body(s, s % 2)
            with eng.Fori(1, (GROUPS - 2) // 2) as k:
                body(k * 2 + 1, 1, True)
                body(k * 2 + 2, 0, True)
            for s in range(GROUPS - 1, GROUPS + 2):
                body(s, s % 2)

        block = ctx.enter_context(nc.Block())

        @block.sync
        def _(sp):
            sp.dma_start(x_all[:, 0:TILES, :], x_tiles[:, 0:TILES, :]).then_inc(x_in[0], 16)
            sp.dma_start(eye, identity).then_inc(consts_in, 16)
            sp.dma_start(colc[:, :], cols).then_inc(consts_in, 16)
            sp.dma_start(wraw[:, :], weights).then_inc(consts_in, 16)
            sp.dma_start(rowc[:, :], rows).then_inc(consts_in, 16)
            sp.dma_start(triangles[:, :], bf16_consts).then_inc(consts_in, 16)
            sp.dma_start(sel[:, :], selectors).then_inc(consts_in, 16)
            sp.dma_start(x_all[:, TILES:2 * TILES, :], x_tiles[:, TILES:2 * TILES, :]).then_inc(x_in[1], 16)
            with sp.Fori(1, GROUPS // 2) as k:
                for i in range(2):
                    sp.wait_ge(x_in[i], k * 16)
                    at = bass.ds((k * 2 + i) * TILES, TILES)
                    sp.dma_start(x_all[:, at, :], x_tiles[:, at, :]).then_inc(x_in[i], 16)
            with sp.Fori(0, GROUPS, 1) as g:
                sp.wait_ge(final_ready, g + 1)
                at = bass.ds(g * TILES, TILES)
                sp.dma_start(out_tiles[:, at, :], x_all[:, at, :]).then_inc(stored, 16)
            sp.wait_ge(stored, 16 * GROUPS)

        @block.tensor
        def _(pe):
            mm = nc.tensor.matmul

            pe.wait_ge(consts_in, 96)
            beta = colc[:, C_BETA:C_BETA + 1]
            for n, at in enumerate((W_Z, W_Z + P, W_BC, W_XD, W_XD + P)):
                mm(misc[:, n:n + 1], wraw[:, at:at + P], beta, start=True, stop=True)
            pe.wait_ge(setup_dve, 1)
            mm(misc[:, P:P + HEADS], gated_xn[:, 0, :], wraw[:, W_XD + INNER:W_XD + XD], start=True, stop=True).then_inc(setup_pe, 1)

            def spread(b, p, h):
                after(pe, scan_done, b * 8 + (h - 1))
                mm(bcast[h % 2][:, :], sel_head[:, h, :], decay_rows[p][0:24, 0:TOK],
                   start=True, stop=True).then_inc(bcast_ps, 1)

            def project_xs(p, c):
                mm(front[2 - c][:, :], w_in[:, W_XD + c * P:W_XD + (c + 1) * P], u_t[p][:, :], start=True, stop=True).then_inc(xst_ps, 1)

            def transpose_xs(p, q):
                for t in (2 * q, 2 * q + 1):
                    for c in range(HALVES):
                        at = (t % 2) * INNER + c * P
                        last = nc.tensor.transpose(front[2 * q][:, at:at + P], xs_t[p][:, c, t * P:(t + 1) * P], eye)
                last.then_inc(xs_ps, 1)

            def project_dt(p):
                mm(front[0][:, 32:64], share_b[:, :], row_parts[:, 0:HEADS].unsqueeze(1).to_broadcast([BIAS_ROWS, TILES, HEADS]),
                   start=True, stop=True, skip_group_check=True)
                for t in range(TILES):
                    last = mm(front[0][:, 32 + t * HEADS:32 + (t + 1) * HEADS], u_t[p][:, t * P:(t + 1) * P],
                              w_in[:, W_XD + INNER:W_XD + XD], start=False, stop=True, skip_group_check=True)
                last.then_inc(dt_ps, 1)

            def apply_masks(b, p, h0):
                for h in (h0, h0 + 1):
                    if h in POOL_HEADS:
                        pe.wait_ge(mask_pool, b * len(POOL_HEADS) + (POOL_HEADS.index(h) + 1))
                    else:
                        pe.wait_ge(mask_dve, b * len(DVE_HEADS) + (DVE_HEADS.index(h) + 1))
                for t in range(TILES):
                    for h in (h0, h0 + 1):
                        q = 32 * (h % 4)
                        last = mm(y_ps[h // 4][q:q + 32, t * P:(t + 1) * P], dtx[p][:, t, h * HEAD_DIM:(h + 1) * HEAD_DIM],
                                  masks[:, h % SLOTS, t * P:(t + 1) * P], start=False, stop=True, skip_group_check=True)
                        if t == TILES - 1:
                            last.then_inc(y_done, 1)

            def transpose_inputs(g, p):
                pe.wait_ge(uh_ready, g * 4 + 4)
                after(pe, g_off_ready, g * 2 - 1)
                for t in range(TILES):
                    last = nc.tensor.transpose(front[2][:, t * P:(t + 1) * P], uh[:, t, :], eye)
                last.then_inc(ut_ps, 1)
                pe.wait_ge(xn_ready, g * 4 + 4)
                after(pe, g_off_ready, g * 2)
                for t in range(TILES):
                    last = nc.tensor.transpose(front[1][:, t * P:(t + 1) * P], xn[p][:, t, :], eye)
                last.then_inc(xnt_ps, 1)

            transpose_inputs(0, 0)
            pe.wait_ge(setup_dve, 2)

            def step(s, p, full=False):
                n, f, b, o = (True,) * 4 if full else (s + 1 < GROUPS, s < GROUPS, 1 <= s <= GROUPS, s >= 2)
                g, gb, go, pb = s, s - 1, s - 2, 1 - p
                if f:
                    pe.wait_ge(ut_ready, g + 1)
                    after(pe, z_done, g * 2 - 1)
                    project_xs(p, 0)
                if b:
                    pe.wait_ge(rows_ready, gb + 1)
                    spread(gb, pb, 0)
                if f:
                    pe.wait_ge(xnt_ready, g + 1)
                    after(pe, z_done, g * 2)
                    project_xs(p, 1)
                if b:
                    spread(gb, pb, 1)
                if f:
                    if not b:
                        pe.wait_ge(setup_dve, 3)
                        project_dt(0)
                        for c in range(HALVES):
                            mm(y_ps[c][:, :], sel[:, 0:P], sel[:, 0:TOK], start=True, stop=True)
                if o:
                    pe.wait_ge(rkv_ready, s if full else min(s, GROUPS))
                    pe.wait_ge(yz_first_ready, go * 2 + 2)
                    mm(misc[:, :], share_b[:, :], row_parts[:, HEADS:HEADS + D].unsqueeze(1).to_broadcast([BIAS_ROWS, TILES, D]),
                       start=True, stop=True, skip_group_check=True)
                    for t in (0, 2, 1, 3):
                        if t == 1:
                            pe.wait_ge(yz_second_ready, go + 1)
                        for c in range(HALVES):
                            at = W_O + c * D
                            last = mm(misc[:, t * P:(t + 1) * P], yz[:, c, t * P:(t + 1) * P], wraw[:, at:at + D],
                                      start=False, stop=True, skip_group_check=True)
                    last.then_inc(out_ps, 1)
                if b:
                    spread(gb, pb, 2)
                if f:
                    pe.wait_ge(xst_ready, g * 2 + 2)
                    after(pe, rows_ready, g)
                    pe.wait_ge(dt_abs_ready, g + 1)
                    transpose_xs(p, 0)
                    transpose_xs(p, 1)
                    mm(front[1][:, :], w_in[:, W_BC:W_BC + P], u_t[p][:, :], start=True, stop=True).then_inc(bc_ps, 1)
                if b:
                    spread(gb, pb, 3)
                    pe.wait_ge(dtx_ready, gb + 1)
                    pe.wait_ge(skip_done, gb * 2 + 1)
                    apply_masks(gb, pb, 0)
                if f:
                    pe.wait_ge(xs_ready, g * 2 + 1)
                    pe.wait_ge(xk_ready, g + 1)
                    mm(front[0][:, :], wraw[:, W_K:W_K + P], xk_t[:, :, :], start=True, stop=True).then_inc(k_ps, 1)
                if b:
                    if o:
                        pe.wait_ge(gated_out_ready, go + 1)
                    else:
                        pe.wait_ge(rkv_ready, gb + 1)
                    for c in range(HALVES):
                        last = mm(misc[:, c * 2 * P:(c + 1) * 2 * P], sel_half[:, c, :], decay_rows[pb][0:24, TOK:TOK + SEQS * P],
                                  start=True, stop=True)
                    last.then_inc(p_ps, 1)
                    spread(gb, pb, 4)
                if f:
                    pe.wait_ge(xs_ready, g * 2 + 2)
                    pe.wait_ge(bc_ready, g * 2 + 2)
                    for q in range(SEQS):
                        a = q * SEQ
                        mm(front[2 - q][:, 0:SEQ], b_t[:, a:a + P], c_t[:, a:a + SEQ], start=True, stop=True)
                        mm(front[2 - q][:, SEQ:SEQ + P], b_t[:, a + P:a + SEQ], c_t[:, a + P:a + SEQ],
                           start=True, stop=True).then_inc(g_ps, 1)
                if b:
                    spread(gb, pb, 5)
                    pe.wait_ge(p_ready, gb + 1)
                    pe.wait_ge(dtx_r_ready, gb + 1)
                    pe.wait_ge(g_off_ready, gb * 2 + 2)
                    for c in range(HALVES):
                        for q in range(SEQS):
                            last = mm(misc[:, (c * SEQS + q) * P:(c * SEQS + q + 1) * P], dtx_r[pb][:, q, c * P:(c + 1) * P],
                                      g_off[pb][:, q, :], start=True, stop=True)
                    last.then_inc(off_ps, 1)
                if f:
                    pe.wait_ge(xr_ready, g + 1)
                    pe.wait_ge(k_relu_ready, g + 1)
                    for t in range(TILES):
                        last = mm(front[0][:, t * P:(t + 1) * P], xr_t[:, t // 2, (t % 2) * P:(t % 2 + 1) * P],
                                  wraw[:, W_R:W_R + P], start=True, stop=True)
                    last.then_inc(r_ps, 1)
                if b:
                    apply_masks(gb, pb, 2)
                    spread(gb, pb, 6)
                if n:
                    transpose_inputs(g + 1, 1 - p)
                if b:
                    spread(gb, pb, 7)
                if n:
                    pe.wait_ge(r_tanh_ready, g + 1)
                    pe.wait_ge(ut_ready, g + 2)
                    project_dt(1 - p)
                if f:
                    pe.wait_ge(r_tanh_ready, g + 1)
                    pe.wait_ge(dt_parts_ready, g + 1)
                    for m, (mask, t0) in enumerate(((upto_b, 1), (after_b, 0))):
                        for part in range(3):
                            last = mm(front[0][:, m * 16:m * 16 + 16], mask, dt_a_parts[:, part, t0:TILES:2, :],
                                      start=(part == 0), stop=(part == 2))
                    last.then_inc(sums_ps, 1)
                if b:
                    pe.wait_ge(skip_done, gb * 2 + 2)
                    apply_masks(gb, pb, 4)
                if f:
                    if n:
                        pe.wait_ge(ut_ready, g + 2)
                    else:
                        pe.wait_ge(g_off_ready, g * 2 + 1)
                    mm(front[2][:, :], w_in[:, W_Z:W_Z + P], u_t[p][:, :], start=True, stop=True).then_inc(z_ps, 1)
                if b:
                    apply_masks(gb, pb, 6)
                if f:
                    if n:
                        pe.wait_ge(xnt_ready, g + 2)
                    else:
                        pe.wait_ge(g_off_ready, g * 2 + 2)
                    mm(front[1][:, :], w_in[:, W_Z + P:W_Z + 2 * P], u_t[p][:, :], start=True, stop=True).then_inc(z_ps, 1)
                    pe.wait_ge(parts_ready, g + 1)
                    pe.wait_ge(decays_ready, g * 2 + 2)
                    if n:
                        pe.wait_ge(dt_abs_ready, g + 2)
                    for t in range(TILES + SEQS):
                        last = nc.tensor.transpose(rows_ps[:, t * P:(t + 1) * P], decay_parts[:, t, :], eye_b)
                    last.then_inc(rows_done, 1)
                    if b:
                        pe.wait_ge(off_ready, gb + 1)
                    pe.wait_ge(k_act_ready, g + 1)
                    for t in range(TILES):
                        last = mm(misc[:, t * P:(t + 1) * P], k_act[:, t * P:(t + 1) * P], w_v[:, :], start=True, stop=True)
                    last.then_inc(v_ps, 1)

            steps(pe, step)

        @block.scalar
        def _(act):
            fn = nc.scalar.activation
            act.wait_ge(consts_in, 96)
            fn(neg_a[:, :], rowc[:, R_ALOG:R_ALOG + HEADS], ACT.Exp).then_inc(setup_act, 1)

            def normalise(g, p):
                act.wait_ge(xc_ready, g + 1)
                act.wait_ge(rstd_ready, g + 1)
                after(act, gated_xn_ready, g - 1)
                for t in range(TILES):
                    fn(xn[p][:, t, :], xc[:, t, :], ACT.Copy, scale=rstd[:, 0, t:t + 1]).then_inc(xn_ready, 1)

            def inputs_transposed(g, p):
                act.wait_ge(ut_ps, g + 1)
                fn(u_t[p][:, :], front[2][:, :], ACT.Copy).then_inc(ut_ready, 1)
                act.wait_ge(xnt_ps, g + 1)
                after(act, xk_ready, g)
                after(act, xr_ready, g)
                fn(xn_t[:, :, 1:SEQ + 1], front[1][:, :].rearrange("p (q t) -> p q t", q=SEQS), ACT.Copy).then_inc(xnt_ready, 1)

            normalise(0, 0)
            inputs_transposed(0, 0)
            act.wait_ge(setup_dve, 3)

            def dt_exponential(g):
                act.wait_ge(dt_ps, g + 1)
                after(act, dt_ready, g)
                raw = front[0][:, 32:64].rearrange("p (t h) -> p t h", h=HEADS)
                fn(dt_raw[:, :, :], raw, ACT.Copy)
                fn(dt_abs[:, :, :], raw, ACT.Abs).then_inc(dt_abs_ready, 1)
                act.wait_ge(dt_abs_ready, g + 1)
                fn(dt_exp[:, :, :], dt_abs[:, :, :], ACT.Exp, scale=-1.0).then_inc(dt_exp_ready, 1)

            def step(s, p, full=False):
                n, f, b = (True,) * 3 if full else (s + 1 < GROUPS, s < GROUPS, 1 <= s <= GROUPS)
                g, gb, pb = s, s - 1, 1 - p
                if f:
                    for c in range(HALVES):
                        act.wait_ge(xst_ps, g * 2 + c + 1)
                        fn(xs_t[p][:, c, :], front[2 - c][:, :], ACT.Identity, bias=bias_col[:, 3 + c:4 + c]).then_inc(xst_ready, 1)
                    if not b:
                        dt_exponential(0)
                if b:
                    act.wait_ge(rkv_ready, gb + 1)
                    after(act, gated_out_ready, gb - 1)
                    fn(gate[pb][:, :], rkv[:, :], ACT.Silu).then_inc(gate_ready, 1)
                    act.wait_ge(xst_ready, gb * 2 + 2)
                    after(act, yz_first_ready, gb * 2)
                    after(act, y_sum_ready, gb * 2)
                    for c in range(HALVES):
                        fn(y_ps[c][:, :], xs_t[pb][:, c, :], ACT.Copy, scale=colc[:, C_DSK + c:C_DSK + c + 1]).then_inc(skip_done, 1)
                if f:
                    after(act, dtx_ready, g)
                    for q in range(SEQS):
                        act.wait_ge(xs_ps, g * 2 + q + 1)
                        fn(xs[:, 2 * q:2 * q + 2, :], front[2 * q][:, :].rearrange("p (t i) -> p t i", t=2), ACT.Copy).then_inc(xs_ready, 1)
                    act.wait_ge(bc_ps, g + 1)
                    after(act, g_ps, g * 2)
                    fn(b_t[:, :], front[1][0:STATE, :], ACT.Identity, bias=bias_col[0:STATE, 2:3]).then_inc(bc_ready, 1)
                    fn(c_t[:, :], front[1][STATE:P, :], ACT.Identity, bias=bias_col[STATE:P, 2:3]).then_inc(bc_ready, 1)
                    fn(table_warm[:, 1:2], neg_a[:, 0:1], ACT.Exp)
                    act.wait_ge(k_ps, g + 1)
                    fn(k_relu[:, :], front[0][:, :], ACT.Relu).then_inc(k_relu_ready, 1)
                    act.wait_ge(dt_a_ready, g + 1)
                    after(act, parts_ready, g)
                    after(act, dtx_r_ready, g)
                    fn(decays[:, 0:TILES, :], dt_a[:, :, :], ACT.Exp, bias=colc[:, C_RESET:C_RESET + 1]).then_inc(decays_ready, 1)
                if b:
                    act.wait_ge(p_ps, gb + 1)
                    after(act, off_ready, gb)
                    fn(p_bc[:, :, :, :], misc[:, :].rearrange("p (c q t) -> p c q t", c=HALVES, q=SEQS), ACT.Copy).then_inc(p_ready, 1)
                if n:
                    normalise(g + 1, 1 - p)
                if f:
                    after(act, mask_dve, (g - 1) * len(DVE_HEADS))
                    after(act, mask_pool, (g - 1) * len(POOL_HEADS))
                    after(act, off_ps, g - 1)
                    for q in range(SEQS):
                        act.wait_ge(g_ps, g * 2 + q + 1)
                        products = front[2 - q][:, :].rearrange("p (t i) -> p t i", i=SEQ)
                        fn(g_diag[p][:, 2 * q:2 * q + 2, :], products[:, :, 0:P], ACT.Copy).then_inc(g_diag_ready, 1)
                        fn(g_off[p][:, q, :], products[:, 0, P:SEQ], ACT.Copy).then_inc(g_off_ready, 1)
                    act.wait_ge(k_relu_ready, g + 1)
                    after(act, v_ps, g)
                    fn(k_act[:, :], k_relu[:, :], ACT.Square).then_inc(k_act_ready, 1)
                    act.wait_ge(r_ps, g + 1)
                    after(act, rkv_ready, g)
                    fn(r_tanh[:, :], front[0][:, :], ACT.Tanh, scale=0.5).then_inc(r_tanh_ready, 1)
                if n:
                    inputs_transposed(g + 1, 1 - p)
                if f:
                    act.wait_ge(sums_ps, g + 1)
                    fn(decays[:, TILES:TILES + 2 * SEQS, :], front[0][:, 0:32].rearrange("p (t h) -> p t h", h=HEADS),
                       ACT.Exp).then_inc(decays_ready, 1)
                if n:
                    dt_exponential(g + 1)
                if f:
                    fn(table_warm[:, 0:1], neg_a[:, 0:1], ACT.Silu)
                    after(act, yz_second_ready, g - 1)
                    act.wait_ge(z_ps, g * 2 + 1)
                    fn(z_silu[p][:, 0, :], front[2][:, :], ACT.Silu, bias=bias_col[:, 0:1]).then_inc(z_done, 1)
                    act.wait_ge(z_ps, g * 2 + 2)
                    fn(z_silu[p][:, 1, :], front[1][:, :], ACT.Silu, bias=bias_col[:, 1:2]).then_inc(z_done, 1)
                    act.wait_ge(rows_done, g + 1)
                    after(act, bcast_ps, (g - 1) * 8)
                    after(act, p_ps, g - 1)
                    fn(decay_rows[p][:, :], rows_ps, ACT.Copy).then_inc(rows_ready, 1)

            steps(act, step)

        @block.gpsimd
        def _(pool):
            tt = nc.gpsimd.tensor_tensor
            nc.gpsimd.memset(xn_t[:, :, 0:1], 0.0)
            nc.gpsimd.memset(zeros[:, :, :], 0.0)
            nc.gpsimd.memset(share_b[:, :], 1 / 32)
            nc.gpsimd.memset(decay_parts[:, :, 24:32], 0.0)
            nc.gpsimd.memset(minus_half[:, :, :], -0.5).then_inc(setup_pool, 1)
            pool.wait_ge(setup_pool, 1)

            def inverse_deviations(g):
                at = bass.ds(g * TILES, TILES)
                pool.wait_ge(norm_chain, g * 9 + 9)
                after(pool, xn_ready, g * 4)
                tt(xc[:, :, :], x_all[:, at, :], mean[:, :].unsqueeze(2).to_broadcast([P, TILES, D]), ALU.subtract).then_inc(xc_ready, 1)
                pool.wait_ge(var_ready, g * 2 + 2)
                after(pool, uh_ready, g * 4)
                tt(rstd[:, :, :], variances[:, :, :], minus_half[:, :, :], ALU.pow).then_inc(rstd_ready, 1)

            def mask_head(b, p, h):
                pool.wait_ge(scan_done, b * 8 + h + 1)
                pool.wait_ge(g_diag_ready, b * 2 + 2)
                tt(masks[:, h % SLOTS, :], masks[:, h % SLOTS, :], g_diag[p][:, :, :].rearrange("p t i -> p (t i)"),
                   ALU.mult).then_inc(mask_pool, 1)

            def difference(g):
                pool.wait_ge(xnt_ready, g + 1)
                after(pool, xk_ready, g)
                after(pool, xr_ready, g)
                tt(diff[:, :, :], xn_t[:, :, 1:SEQ + 1], xn_t[:, :, 0:SEQ], ALU.subtract).then_inc(diff_ready, 1)

            inverse_deviations(0)
            pool.wait_ge(consts_in, 96)
            for t in range(1, TILES):
                last = nc.gpsimd.tensor_copy(eye4[:, t * P:(t + 1) * P], eye)
            last.then_inc(setup_pool, 1)
            difference(0)

            def step(s, p, full=False):
                n, f, b, o = (True,) * 4 if full else (s + 1 < GROUPS, s < GROUPS, 1 <= s <= GROUPS, s >= 2)
                g, gb, go, pb = s, s - 1, s - 2, 1 - p
                if o:
                    pool.wait_ge(y_sum_ready, go * 2 + 2)
                    pool.wait_ge(z_done, go * 2 + 2)
                    after(pool, out_ps, go)
                    for c in range(HALVES):
                        at = yz[:, c, :].rearrange("p (q a i) -> p q a i", q=SEQS, a=2)[:, :, 1, :]
                        z = z_silu[p][:, c, :].rearrange("p (q a i) -> p q a i", q=SEQS, a=2)[:, :, 1, :]
                        last = tt(at, y_sum[:, c, :, :], z, ALU.mult)
                    last.then_inc(yz_second_ready, 1)
                if b:
                    pool.wait_ge(gate_ready, gb + 1)
                    tt(gated_xn[:, :, :], xn[pb][:, :, :], gate[pb][:, :].rearrange("p (t d) -> p t d", d=D),
                       ALU.mult).then_inc(gated_xn_ready, 1)
                    mask_head(gb, pb, 1)
                if n:
                    inverse_deviations(g + 1)
                if b:
                    mask_head(gb, pb, 3)
                if f:
                    pool.wait_ge(dt_ready, g + 1)
                    pool.wait_ge(xs_ready, g * 2 + 2)
                    after(pool, y_done, (g - 1) * 8)
                    for t in range(TILES):
                        last = tt(dtx[p][:, t, :].rearrange("p (h e) -> p h e", h=HEADS),
                                  xs[:, t, :].rearrange("p (h e) -> p h e", h=HEADS),
                                  dt[:, t, :].unsqueeze(2).to_broadcast([P, HEADS, HEAD_DIM]), ALU.mult)
                    last.then_inc(dtx_ready, 1)
                if b:
                    mask_head(gb, pb, 5)
                    pool.wait_ge(gated_xn_ready, gb + 1)
                    x_b = x_all[:, bass.ds(gb * TILES, TILES), :]
                    tt(x_b, gated_xn[:, :, :], x_b, ALU.add).then_inc(residual_ready, 1)
                if f:
                    pool.wait_ge(decays_ready, g * 2 + 2)
                    after(pool, rows_done, g)
                    wide, part = decays[:, 0:TILES + SEQS, :], decay_parts
                    tt(part[:, :, 0:8], wide, zeros[:, :, :], ALU.add).then_inc(split_chain, 1)
                    pool.wait_ge(split_chain, g * 3 + 1)
                    tt(decays_rest[:, :, :], wide, part[:, :, 0:8], ALU.subtract).then_inc(split_chain, 1)
                    pool.wait_ge(split_chain, g * 3 + 2)
                    tt(part[:, :, 8:16], decays_rest[:, :, :], zeros[:, :, :], ALU.add).then_inc(split_chain, 1)
                    pool.wait_ge(split_chain, g * 3 + 3)
                    tt(part[:, :, 16:24], decays_rest[:, :, :], part[:, :, 8:16], ALU.subtract).then_inc(parts_ready, 1)
                if n:
                    difference(g + 1)
                if f:
                    pool.wait_ge(dtx_ready, g + 1)
                    after(pool, off_ps, g - 1)
                    for q in range(SEQS):
                        last = tt(dtx_r[p][:, q, :].rearrange("p (h e) -> p h e", h=HEADS),
                                  dtx[p][:, 2 * q, :].rearrange("p (h e) -> p h e", h=HEADS),
                                  decays[:, TILES + SEQS + q, :].unsqueeze(2).to_broadcast([P, HEADS, HEAD_DIM]), ALU.mult)
                    last.then_inc(dtx_r_ready, 1)

            steps(pool, step)

        @block.vector
        def _(dve):
            v = nc.vector
            SETUP = 10

            def norm_stats(g, i, t):
                if t == 0:
                    dve.wait_ge(x_in[i], g * 8 + (16 - 8 * i))
                    after(dve, norm_chain, g * 9)
                v.bn_stats(stats[:, t, :], x_all[:, bass.ds(g * TILES + t, 1), :].rearrange("p o d -> p (o d)")).then_inc(norm_chain, 1)

            m_even, q_even, m_odd, q_odd = (stats[:, :, k] for k in (1, 2, 4, 5))

            def norm_gaps(g):
                dve.wait_ge(norm_chain, g * 9 + 4)
                v.tensor_tensor(m_gap[:, :], m_even, m_odd, ALU.subtract).then_inc(norm_chain, 1)
                v.tensor_tensor(q_sum[:, :], q_even, q_odd, ALU.add).then_inc(norm_chain, 1)

            def norm_mean(g):
                dve.wait_ge(norm_chain, g * 9 + 6)
                after(dve, uh_ready, g * 4)
                after(dve, xc_ready, g)
                v.scalar_tensor_tensor(out=mean[:, :], in0=m_gap[:, :], scalar=-0.5, in1=m_even,
                                       op0=ALU.mult, op1=ALU.add).then_inc(norm_chain, 1)
                v.tensor_tensor(m_gap2[:, :], m_gap[:, :], m_gap[:, :], ALU.mult).then_inc(norm_chain, 1)

            def norm_deviations(g):
                dve.wait_ge(norm_chain, g * 9 + 8)
                v.scalar_tensor_tensor(out=q_all[:, :], in0=m_gap2[:, :], scalar=D / 4.0, in1=q_sum[:, :],
                                       op0=ALU.mult, op1=ALU.add).then_inc(norm_chain, 1)

            def norm_variances(g):
                dve.wait_ge(norm_chain, g * 9 + 9)
                v.tensor_scalar(variances[:, 0, :], q_all[:, :], 1.0 / D, EPS, ALU.mult, ALU.add).then_inc(var_ready, 1)
                v.tensor_scalar(variances[:, 1, :], q_all[:, :], (1.0 + EPS) / D, EPS * EPS, ALU.mult, ALU.add).then_inc(var_ready, 1)

            def normalise(g, p):
                dve.wait_ge(rstd_ready, g + 1)
                after(dve, ut_ps, g)
                for t in range(TILES):
                    v.tensor_scalar(uh[:, t, :], x_all[:, bass.ds(g * TILES + t, 1), :].rearrange("p o d -> p (o d)"),
                                    mean[:, t:t + 1], rstd[:, 1, t:t + 1], ALU.subtract, ALU.mult).then_inc(uh_ready, 1)

            def scan(b, h):
                dve.wait_ge(bcast_ps, b * 8 + h + 1)
                after(dve, y_done, b * 8 + (h + 1 - SLOTS))
                v.tensor_tensor_scan(masks[:, h % SLOTS, :], bcast[h % 2][:, :], eye4, 0.0, ALU.mult, ALU.add).then_inc(scan_done, 1)

            def mask_head(b, p, h):
                dve.wait_ge(scan_done, b * 8 + h + 1)
                dve.wait_ge(g_diag_ready, b * 2 + 2)
                v.tensor_tensor(masks[:, h % SLOTS, :], masks[:, h % SLOTS, :],
                                g_diag[p][:, :, :].rearrange("p t i -> p (t i)"), ALU.mult).then_inc(mask_dve, 1)

            def log1p(g, k):
                done = LOG1P_DEG - k
                q, e = poly[:, k % 2, :, :], dt_exp[:, :, :]
                if k == LOG1P_DEG:
                    dve.wait_ge(dt_exp_ready, g + 1)
                    v.tensor_scalar(q, e, coef[k], None, ALU.mult).then_inc(dt_chain, 1)
                else:
                    dve.wait_ge(dt_chain, g * 12 + (SETUP + done))
                    v.scalar_tensor_tensor(out=q, in0=poly[:, (k + 1) % 2, :, :], scalar=coef[k], in1=e,
                                           op0=ALU.add, op1=ALU.mult).then_inc(dt_chain, 1)

            def dt_value(g):
                dve.wait_ge(dt_chain, g * 12 + (SETUP + LOG1P_DEG + 1))
                v.scalar_tensor_tensor(out=dt[:, :, :], in0=dt_raw[:, :, :], scalar=0.0, in1=poly[:, 0, :, :],
                                       op0=ALU.max, op1=ALU.add).then_inc(dt_ready, 1)

            def dt_decay(g):
                dve.wait_ge(dt_ready, g + 1)
                after(dve, decays_ready, g * 2)
                v.tensor_tensor(dt_a[:, :, :], dt[:, :, :], neg_a[:, :].unsqueeze(1).to_broadcast([P, TILES, HEADS]),
                                ALU.mult).then_inc(dt_a_ready, 1)

            def dt_part(g, n):
                part, rest = dt_a_parts, dt_a_rest[:, :, :]
                if n == 0:
                    dve.wait_ge(dt_a_ready, g + 1)
                    after(dve, sums_ps, g)
                    v.tensor_copy(part[:, 0, :, :], dt_a[:, :, :]).then_inc(dt_chain, 1)
                else:
                    dve.wait_ge(dt_chain, g * 12 + (SETUP + LOG1P_DEG + 1 + n))
                if n == 1:
                    v.tensor_tensor(rest, dt_a[:, :, :], part[:, 0, :, :], ALU.subtract).then_inc(dt_chain, 1)
                if n == 2:
                    v.tensor_copy(part[:, 1, :, :], rest).then_inc(dt_chain, 1)
                if n == 3:
                    v.tensor_tensor(part[:, 2, :, :], rest, part[:, 1, :, :], ALU.subtract).then_inc(dt_parts_ready, 1)

            def mix(g, mu, dst, done, used):
                dve.wait_ge(diff_ready, g + 1)
                after(dve, used, g)
                v.scalar_tensor_tensor(out=dst[:, :, :], in0=diff[:, :, :], scalar=colc[:, mu:mu + 1], in1=xn_t[:, :, 0:SEQ],
                                       op0=ALU.mult, op1=ALU.add).then_inc(done, 1)

            def read_y(b, p):
                dve.wait_ge(y_done, b * 8 + 8)
                dve.wait_ge(off_ready, b + 1)
                dve.wait_ge(z_done, b * 2 + 2)
                after(dve, out_ps, b)
                after(dve, yz_second_ready, b)
                for c in range(HALVES):
                    y = y_ps[c][:, :].rearrange("p (q a i) -> p q a i", q=SEQS, a=2)
                    z = z_silu[p][:, c, :].rearrange("p (q a i) -> p q a i", q=SEQS, a=2)
                    dst = yz[:, c, :].rearrange("p (q a i) -> p q a i", q=SEQS, a=2)
                    v.tensor_tensor(y_sum[:, c, :, :], y[:, :, 1, :], y_off[:, c, :, :], ALU.add).then_inc(y_sum_ready, 1)
                    v.tensor_tensor(dst[:, :, 0, :], y[:, :, 0, :], z[:, :, 0, :], ALU.mult).then_inc(yz_first_ready, 1)

            def gate_output(o, p):
                dve.wait_ge(out_ps, o + 1)
                dve.wait_ge(gate_ready, o + 1)
                v.tensor_tensor(gated_out[:, :], misc[:, :], gate[p][:, :], ALU.mult).then_inc(gated_out_ready, 1)

            def add_residual(o):
                dve.wait_ge(gated_out_ready, o + 1)
                dve.wait_ge(residual_ready, o + 1)
                x_o = x_all[:, bass.ds(o * TILES, TILES), :]
                v.tensor_tensor(x_o, gated_out[:, :].rearrange("p (t d) -> p t d", d=D), x_o, ALU.add).then_inc(final_ready, 1)

            def scale_off(b):
                dve.wait_ge(off_ps, b + 1)
                dve.wait_ge(p_ready, b + 1)
                after(dve, y_sum_ready, b * 2)
                v.tensor_tensor(y_off[:, :, :, :].rearrange("p c q i -> p (c q i)"), misc[:, :],
                                p_bc[:, :, :, :].rearrange("p c q i -> p (c q i)"), ALU.mult).then_inc(off_ready, 1)

            def multiply_rkv(g):
                dve.wait_ge(v_ps, g + 1)
                dve.wait_ge(r_tanh_ready, g + 1)
                after(dve, gate_ready, g)
                v.scalar_tensor_tensor(out=rkv[:, :], in0=r_tanh[:, :], scalar=1.0, in1=misc[:, :],
                                       op0=ALU.add, op1=ALU.mult).then_inc(rkv_ready, 1)

            for t in range(TILES):
                norm_stats(0, 0, t)
            norm_gaps(0)
            norm_mean(0)
            norm_deviations(0)
            norm_variances(0)

            dve.wait_ge(consts_in, 96)
            v.tensor_copy(gated_xn[:, 0, :], colc[:, C_BETA:C_BETA + 1].to_broadcast([P, P])).then_inc(setup_dve, 1)
            v.tensor_scalar(w_in[:, :], wraw[:, 0:W_K], colc[:, C_GAMMA:C_GAMMA + 1], None, ALU.mult).then_inc(setup_dve, 1)
            v.tensor_scalar(w_v[:, :], wraw[:, W_V:W_V + D], 0.5, None, ALU.mult)
            v.tensor_copy(row_rest[:, HEADS:], rowc[0:BIAS_ROWS, R_BOUT:R_BOUT + D])
            dve.wait_ge(setup_act, 1)
            v.tensor_scalar(neg_a[:, :], neg_a[:, :], -1.0, None, ALU.mult)
            normalise(0, 0)
            dve.wait_ge(setup_pe, 1)
            v.tensor_tensor(bias_col[:, 0:5], misc[:, 0:5], colc[:, C_BZ:C_BZ + 5], ALU.add).then_inc(dt_chain, 1)
            v.tensor_tensor(row_rest[:, 0:HEADS], misc[0:BIAS_ROWS, P:P + HEADS], rowc[0:BIAS_ROWS, R_BDT:R_BDT + HEADS], ALU.add).then_inc(dt_chain, 1)
            dve.wait_ge(dt_chain, 2)
            v.tensor_tensor(row_rest[:, 0:HEADS], row_rest[:, 0:HEADS], rowc[0:BIAS_ROWS, R_DTB:R_DTB + HEADS], ALU.add).then_inc(dt_chain, 1)
            dve.wait_ge(dt_chain, 3)
            v.tensor_copy(row_parts[:, :], row_rest[:, :]).then_inc(dt_chain, 1)
            done = 4
            for n in (1, 2):
                for lanes in (slice(32 * m, 32 * m + 32) for m in range(n, 3)):
                    dve.wait_ge(dt_chain, done)
                    v.tensor_tensor(row_rest[lanes, :], row_rest[lanes, :], row_parts[lanes, :], ALU.subtract).then_inc(dt_chain, 1)
                    dve.wait_ge(dt_chain, done + 1)
                    v.tensor_copy(row_parts[lanes, :], row_rest[lanes, :]).then_inc(dt_chain, 1)
                    done += 2
            assert done == SETUP
            dve.wait_ge(dt_chain, done)
            dve.wait_ge(setup_pool, 2)
            v.tensor_copy(bias_col[:, 5:6], bias_col[:, 4:5]).then_inc(setup_dve, 1)

            def step(s, p, full=False):
                n, f, b, o = (True,) * 4 if full else (s + 1 < GROUPS, s < GROUPS, 1 <= s <= GROUPS, s >= 2)
                g, gb, go, pb = s, s - 1, s - 2, 1 - p
                if n:
                    norm_stats(g + 1, 1 - p, 0)
                    norm_stats(g + 1, 1 - p, 1)
                    norm_stats(g + 1, 1 - p, 2)
                    norm_stats(g + 1, 1 - p, 3)
                if f:
                    log1p(g, 8)
                if n:
                    norm_gaps(g + 1)
                if f:
                    log1p(g, 7)
                if n:
                    norm_mean(g + 1)
                if f:
                    log1p(g, 6)
                if b:
                    scan(gb, 0)
                if n:
                    norm_deviations(g + 1)
                if f:
                    log1p(g, 5)
                if b:
                    scan(gb, 1)
                if n:
                    norm_variances(g + 1)
                if f:
                    log1p(g, 4)
                if b:
                    mask_head(gb, pb, 0)
                if f:
                    log1p(g, 3)
                if b:
                    scan(gb, 2)
                if f:
                    log1p(g, 2)
                    mix(g, C_MUK, xk_t, xk_ready, k_ps)
                    log1p(g, 1)
                    log1p(g, 0)
                if b:
                    mask_head(gb, pb, 2)
                if f:
                    dt_value(g)
                if o:
                    gate_output(go, p)
                if f:
                    dt_decay(g)
                if b:
                    scan(gb, 3)
                if f:
                    dt_part(g, 0)
                    mix(g, C_MUR, xr_t, xr_ready, r_ps)
                    dt_part(g, 1)
                if n:
                    normalise(g + 1, 1 - p)
                if f:
                    dt_part(g, 2)
                if b:
                    scan(gb, 4)
                if f:
                    dt_part(g, 3)
                if b:
                    mask_head(gb, pb, 4)
                    scan(gb, 5)
                    scale_off(gb)
                    scan(gb, 6)
                    mask_head(gb, pb, 6)
                    scan(gb, 7)
                    mask_head(gb, pb, 7)
                if o:
                    add_residual(go)
                if b:
                    read_y(gb, pb)
                if f:
                    multiply_rkv(g)

            steps(dve, step)


def constants():
    k, m = np.indices((P, P))
    part = np.arange(24)[:, None] % HEADS
    sel_head = np.concatenate([np.repeat(part == h, P, axis=1) for h in range(HEADS)], axis=1)
    sel_half = part == (np.arange(INNER) // HEAD_DIM)[None, :]
    b16 = mybir.dt.np(BF16)
    return (np.eye(P, dtype=np.float32), np.concatenate([k == m, k <= m, k > m], axis=1).astype(b16),
            np.concatenate([sel_head, sel_half], axis=1).astype(b16))


def kernel(L0_attn_input_tensor, L0_attn_ln_gamma, L0_attn_ln_beta, L0_attn_W_in, L0_attn_b_in, L0_attn_A_log, L0_attn_D_skip,
           L0_attn_dt_bias, L0_attn_W_out, L0_attn_b_out, L0_ffn_W_r, L0_ffn_W_k, L0_ffn_W_v, L0_ffn_mu_r, L0_ffn_mu_k):
    import concourse.bacc as bacc
    from concourse.bass_utils import run_bass_kernel_spmd

    x = np.ascontiguousarray(np.asarray(L0_attn_input_tensor)).reshape(BATCH * SEQ, D)
    w_in, b_in = np.asarray(L0_attn_W_in), np.asarray(L0_attn_b_in)
    z, xs, bc_, dt = slice(0, INNER), slice(INNER, 2 * INNER), slice(2 * INNER, 2 * INNER + 2 * STATE), slice(2 * INNER + 2 * STATE, None)
    w_out = np.asarray(L0_attn_W_out)
    weights = np.concatenate([w_in[:, z], w_in[:, xs], w_in[:, dt], w_in[:, bc_], np.asarray(L0_ffn_W_k).T, np.asarray(L0_ffn_W_r).T,
                              np.asarray(L0_ffn_W_v).T] + [w_out[c * P:(c + 1) * P] for c in range(HALVES)], axis=1)
    reset = np.zeros(P, np.float32)
    reset[0] = -30000.0
    skip = np.repeat(np.asarray(L0_attn_D_skip), HEAD_DIM)
    cols = np.stack([np.asarray(L0_attn_ln_gamma), np.asarray(L0_attn_ln_beta), np.asarray(L0_ffn_mu_r), np.asarray(L0_ffn_mu_k),
                     b_in[0:P], b_in[P:2 * P], b_in[bc_], b_in[xs][:P], b_in[xs][P:], skip[:P], skip[P:], reset], axis=1)
    row = np.concatenate([b_in[dt], np.asarray(L0_attn_dt_bias), np.asarray(L0_attn_A_log), np.asarray(L0_attn_b_out)])
    rows = np.tile(row[None, :], (P, 1))
    identity, bf16_consts, selectors = constants()
    arrays = {"x": x, "weights": weights, "cols": cols, "rows": rows, "identity": identity, "bf16_consts": bf16_consts,
              "selectors": selectors}
    arrays = {k: np.ascontiguousarray(a) for k, a in arrays.items()}

    nc = bacc.Bacc("TRN2", target_bir_lowering=False, num_devices=1)
    args = [nc.dram_tensor(n, list(a.shape), mybir.dt.from_np(a.dtype), kind="ExternalInput").ap() for n, a in arrays.items()]
    out = nc.dram_tensor("out", [BATCH * SEQ, D], F32, kind="ExternalOutput").ap()
    build(nc, *args, out)
    result = run_bass_kernel_spmd(nc, [arrays], core_ids=[0])
    return result.results[0]["out"].reshape(BATCH, SEQ, D)
```
